# Optimizing a Trainium2 kernel written in Bass

```python
import numpy as np
import jax
import jax.numpy as jnp

def _softmax(x, axis=-1):
    return jax.nn.softmax(x, axis=axis)

def _gelu(x):
    return jax.nn.gelu(x, approximate=True)

def _silu(x):
    return jax.nn.silu(x)

def _sigmoid(x):
    return jax.nn.sigmoid(x)

def _layernorm(x, axis=-1, eps=1e-05):
    m = jnp.mean(x, axis=axis, keepdims=True)
    v = jnp.var(x, axis=axis, keepdims=True)
    return (x - m) / jnp.sqrt(v + eps)

def _scatter_add(tgt, idx, src, axis=0):
    return tgt.at[idx].add(src)

def _segment_sum(src, seg, n):
    return jax.ops.segment_sum(src, seg, n)
kernel_name = 'mk_macaron_d1_jaxref_r8_ac37a9'

def setup_inputs(seed: int=0):
    np.random.seed(seed)
    _w = jnp.asarray

    def _L0_attn_setup():
        import jax, jax.numpy as jnp
        import numpy as np
        D_MODEL = 128
        NUM_HEADS = 16
        D_K = D_MODEL // NUM_HEADS
        BATCH, SEQ = (2, 256)
        key = jax.random.key(seed)
        k = jax.random.split(key, 5)
        std = np.sqrt(2.0 / (D_MODEL + D_MODEL)).astype(np.float32)
        return {'x': jax.random.normal(k[0], (BATCH, SEQ, D_MODEL), dtype=jnp.float32), 'WQ': jax.random.normal(k[1], (D_MODEL, D_MODEL), dtype=jnp.float32) * std, 'WK': jax.random.normal(k[2], (D_MODEL, D_MODEL), dtype=jnp.float32) * std, 'WV': jax.random.normal(k[3], (D_MODEL, D_MODEL), dtype=jnp.float32) * std, 'WO': jax.random.normal(k[4], (D_MODEL, D_MODEL), dtype=jnp.float32) * std}
    _L0_attn_in = _L0_attn_setup()

    def _L0_ffn_setup():
        import jax, jax.numpy as jnp
        import numpy as np
        B, T, D, H, E, TOPK = (2, 256, 128, 256, 8, 2)
        key = jax.random.key(seed)
        ks = jax.random.split(key, 5)
        s_in = 1.0 / np.sqrt(D)
        s_hid = 1.0 / np.sqrt(H)
        return {'x': jax.random.normal(ks[0], (B, T, D), dtype=jnp.float32), 'gate_w': jax.random.normal(ks[1], (E, D), dtype=jnp.float32) * s_in, 'w1': jax.random.normal(ks[2], (E, H, D), dtype=jnp.float32) * s_in, 'w2': jax.random.normal(ks[3], (E, D, H), dtype=jnp.float32) * s_hid, 'w3': jax.random.normal(ks[4], (E, H, D), dtype=jnp.float32) * s_in}
    _L0_ffn_in = _L0_ffn_setup()
    _d = {'L0_attn_x': _L0_attn_in['x'], 'L0_attn_WQ': _L0_attn_in['WQ'], 'L0_attn_WK': _L0_attn_in['WK'], 'L0_attn_WV': _L0_attn_in['WV'], 'L0_attn_WO': _L0_attn_in['WO'], 'L0_ffn_gate_w': _L0_ffn_in['gate_w'], 'L0_ffn_w1': _L0_ffn_in['w1'], 'L0_ffn_w2': _L0_ffn_in['w2'], 'L0_ffn_w3': _L0_ffn_in['w3']}
    _x0 = _d['L0_attn_x']
    _d['L0_attn_x'] = jax.random.normal(jax.random.fold_in(jax.random.key(seed), 1), (16, 256, 128), dtype=_x0.dtype)
    del _x0
    return _d

def reference(L0_attn_x, L0_attn_WQ, L0_attn_WK, L0_attn_WV, L0_attn_WO, L0_ffn_gate_w, L0_ffn_w1, L0_ffn_w2, L0_ffn_w3):

    def _L0_attn_ref(x, WQ, WK, WV, WO):
        import jax, jax.numpy as jnp
        import numpy as np
        D_MODEL = 128
        NUM_HEADS = 16
        D_K = D_MODEL // NUM_HEADS
        BATCH, SEQ = (2, 256)
        B, S, E = x.shape
        mask = jnp.where(jnp.triu(jnp.ones((S, S), dtype=bool), k=1), -jnp.inf, 0.0).astype(x.dtype)

        def heads(W):
            return (x @ W).reshape(B, S, NUM_HEADS, D_K).transpose(0, 2, 1, 3)
        Q, K, V = (heads(WQ), heads(WK), heads(WV))
        score = jnp.einsum('bhqd,bhkd->bhqk', Q, K) / jnp.sqrt(jnp.asarray(D_K, x.dtype))
        score = score + mask
        score = score - jnp.max(score, axis=-1, keepdims=True)
        score = jnp.exp(score)
        score = score / jnp.sum(score, axis=-1, keepdims=True)
        out = jnp.einsum('bhqk,bhkd->bhqd', score, V)
        out = out.transpose(0, 2, 1, 3).reshape(B, S, E)
        return out @ WO

    def _L0_ffn_ref(x, gate_w, w1, w2, w3):
        import jax, jax.numpy as jnp
        import numpy as np
        B, T, D, H, E, TOPK = (2, 256, 128, 256, 8, 2)
        b, t, d = x.shape
        flat = x.reshape(-1, d)
        probs = jax.nn.softmax(flat @ gate_w.T, axis=-1)
        weights, idx = jax.lax.top_k(probs, TOPK)
        weights = weights / jnp.sum(weights, axis=-1, keepdims=True)
        combine = jnp.sum(jax.nn.one_hot(idx, E, dtype=flat.dtype) * weights[..., None], axis=1)
        h1 = jnp.einsum('nd,ehd->neh', flat, w1)
        h3 = jnp.einsum('nd,ehd->neh', flat, w3)
        y = jnp.einsum('neh,edh->ned', jax.nn.silu(h1) * h3, w2)
        out = jnp.einsum('ned,ne->nd', y, combine)
        return out.reshape(b, t, d)
    x = L0_attn_x
    x = x + 0.5 * _L0_ffn_ref(_layernorm(x, axis=-1), L0_ffn_gate_w, L0_ffn_w1, L0_ffn_w2, L0_ffn_w3)
    x = x + _L0_attn_ref(_layernorm(x, axis=-1), L0_attn_WQ, L0_attn_WK, L0_attn_WV, L0_attn_WO)
    x = x + 0.5 * _L0_ffn_ref(_layernorm(x, axis=-1), L0_ffn_gate_w, L0_ffn_w1, L0_ffn_w2, L0_ffn_w3)
    return x

_drawn_inputs = setup_inputs


def setup_inputs(seed=0):
    import zlib

    import numpy as np

    out = dict(_drawn_inputs(seed))
    spreads = {}
    factors = {}
    for name, (base, spread) in spreads.items():
        noise = np.random.default_rng([zlib.crc32(name.encode()), seed]).standard_normal(out[name].shape)
        drawn = base * np.exp(spread * noise) if base else spread * noise
        out[name] = jnp.asarray(drawn.astype(out[name].dtype))
    for name, factor in factors.items():
        out[name] = (out[name] * factor).astype(out[name].dtype)
    return out
```

```python
from contextlib import ExitStack

import numpy as np

import concourse.bass as bass
from concourse import mybir

F32 = mybir.dt.float32
F16 = mybir.dt.float16
BF16 = mybir.dt.bfloat16
ALU = mybir.AluOpType
ACT = mybir.ActivationFunctionType
AX = mybir.AxisListType

P = 128
D = 128
SEQ = 256
HEADS, DK = 16, 8
E, HID = 8, 256
TILES = 4
GTOK = TILES * P
CHUNKS = E * HID // P
LAG = 3
HG = 4
WSCALE = 256.0
EPS = 1e-5
NEG = -1.0e30
MLIMIT = 60000.0
SM_SCALE = DK ** -0.5
GATE_STEPS = 17

D_H = 2
D_HID = 4
D_Y = 2
D_S = 2
D_ST = 3
D_PT = 4
D_O = 1


def freed(n):
    return n + 1


def done(n, depth=0):
    return n + 1 + depth


def build_macaron(nc, x_in, w_up1, w_up3, w_down, w_small, out, batches):
    groups = batches * SEQ // GTOK
    pairs = groups // 2
    assert groups == 2 * pairs and pairs >= 3 and batches == 4 * pairs
    ctx = ExitStack()
    with ctx:
        def sb(name, shape, dt):
            return ctx.enter_context(nc.sbuf_tensor(name, shape, dt))

        def sem(name):
            return ctx.enter_context(nc.semaphore(name))

        X = sb("X", [P, groups * TILES * D], F32)
        w1h = sb("w1h", [P, E * HID], F16)
        w1l = sb("w1l", [P, E * HID], F16)
        w3h = sb("w3h", [P, E * HID], F16)
        w3l = sb("w3l", [P, E * HID], F16)
        w2h = sb("w2h", [P, CHUNKS, D], F16)
        w2l = sb("w2l", [P, CHUNKS, D], F16)
        NSMALL = 4 * D + E
        wsh = sb("wsh", [P, NSMALL], F16)
        wsl = sb("wsl", [P, NSMALL], F16)
        wsmall_f = sb("wsmall_f", [P, NSMALL], F32)
        ident = sb("ident", [P, P], F32)
        ident_h = sb("ident_h", [P, P], F16)
        ident_b = sb("ident_b", [P, P], BF16)
        causal = sb("causal", [P, 4, P], BF16)
        rank = sb("rank", [P, TILES, E], F32)
        stats = sb("stats", [P, TILES, 6], F32)
        meanvar = sb("meanvar", [P, TILES, 2], F32)
        var_eps = sb("var_eps", [P, TILES], F32)
        minus_half = sb("minus_half", [P, TILES], F32)
        rstd = sb("rstd", [P, TILES], F32)
        xn = sb("xn", [P, TILES, D], F32)
        xh = sb("xh", [P, 2, GTOK], F16)
        xl = sb("xl", [P, 2, GTOK], F16)
        silu = sb("silu", [P, D_H, GTOK], F32)
        prod = sb("prod", [P, D_H, GTOK], F32)
        hidh = sb("hidh", [P, D_HID, GTOK], F16)
        hidl = sb("hidl", [P, D_HID, GTOK], F16)
        logit = sb("logit", [P, TILES, E], F32)
        masked = sb("masked", [P, TILES, E], F32)
        score = sb("score", [P, TILES, E], F32)
        hot1 = sb("hot1", [P, TILES, E], F32)
        hot2 = sb("hot2", [P, TILES, E], F32)
        top = sb("top", [P, 8, TILES], F32)
        comb = sb("comb", [P, 2, TILES, E], F32)
        qksplit = sb("qksplit", [P, 2, 4, GTOK], F16)
        zc = sb("zc", [P, 2, 2, HG, GTOK], F16)
        zk = sb("zk", [P, 2, HG, 4, GTOK], F16)
        vaug = sb("vaug", [P, 2, TILES, HEADS, 32], F32)
        negmax = sb("negmax", [P, 2, 2, HEADS], F32)
        negmax_h = sb("negmax_h", [P, 2, 2, HEADS], F16)
        pt = sb("pt", [P, D_PT, 3 * 512], F32)
        ot = sb("ot", [P, 2, HG, SEQ], F32)
        rden = sb("rden", [P, 2, HEADS], F32)
        on = sb("on", [P, 2, D], F32)
        oh = sb("oh", [P, SEQ], F16)
        ol = sb("ol", [P, SEQ], F16)
        wstage = pt[:, :, :].rearrange("p a b -> p (a b)").rearrange("p (k n) -> p k n", n=512)

        bank = ctx.enter_context(nc.psum_tensor("bank", [P, 8, 512], F32))
        B_H1, B_H3, B_Y = 0, 2, 4
        B_S, B_ST, B_O = 0, 2, 5
        B_M0, B_M1 = 6, 7

        x_first = sem("x_first")
        x_rest = sem("x_rest")
        small_loaded = sem("small_loaded")
        w_loaded = [sem(f"w_loaded{k}") for k in range(12)]
        w_hi = sem("w_hi")
        w_lo = sem("w_lo")
        consts = sem("consts")
        zeroed = sem("zeroed")
        ln_stats = sem("ln_stats")
        ln_mean = sem("ln_mean")
        eps_added = sem("eps_added")
        rstd_done = sem("rstd_done")
        xn_done = sem("xn_done")
        m0_ready = sem("m0_ready")
        m0_hi = sem("m0_hi")
        m0_freed = sem("m0_freed")
        h1_ready = sem("h1_ready")
        h3_ready = sem("h3_ready")
        silu_done = sem("silu_done")
        prod_done = sem("prod_done")
        hi_done = sem("hi_done")
        lo_done = sem("lo_done")
        y_done = sem("y_done")
        comb_done = sem("comb_done")
        gate_ready = sem("gate_ready")
        gate_step = sem("gate_step")
        gate_diff = sem("gate_diff")
        gate_tanh = sem("gate_tanh")
        s_ready = sem("s_ready")
        s_reduced = sem("s_reduced")
        clamp_done = sem("clamp_done")
        m_placed = sem("m_placed")
        st_ready = sem("st_ready")
        exp_done = sem("exp_done")
        sel_done = sem("sel_done")
        pv_done = sem("pv_done")
        o_copied = sem("o_copied")
        m1_ready = sem("m1_ready")
        m1_freed = sem("m1_freed")
        oh_done = sem("oh_done")
        ol_done = sem("ol_done")
        rden_done = sem("rden_done")
        on_done = sem("on_done")
        x_attn = sem("x_attn")
        zc_done = sem("zc_done")
        zk_done = sem("zk_done")
        out_done = sem("out_done")

        held = sem("held")

        def hold(eng, what, value):
            eng.wait_ge(what, value)
            eng.sem_inc(held, 1)

        block = ctx.enter_context(nc.Block())

        ALLCHUNKS = groups * CHUNKS
        ALLEXP = groups * E

        M0_ATT = groups
        M0_FFN2 = groups + 4 * groups

        def m0_use(phase, g):
            if phase == 0:
                return g
            if phase == 1:
                return M0_ATT + 4 * g
            return M0_FFN2 + g

        def m1_use(b):
            return 5 * b - 3

        M1_TAIL = m1_use(batches) - 1

        @block.sync
        def _(sp):
            xv = x_in.rearrange("(t p) d -> p t d", p=P)
            Xv = X[:, :].rearrange("p (t d) -> p t d", d=D)
            sp.dma_start(Xv[:, 0:TILES, :], xv[:, 0:TILES, :]).then_inc(x_first, 16)
            sp.dma_start(wsmall_f[:, :], w_small).then_inc(small_loaded, 16)
            for k in range(4):
                for n, w in enumerate((w_up1, w_up3, w_down)):
                    sp.dma_start(wstage[:, 3 * k + n, :], w[:, k * 512:(k + 1) * 512])\
                        .then_inc(w_loaded[3 * k + n], 16)
            for g in range(1, groups):
                sp.dma_start(Xv[:, g * TILES:(g + 1) * TILES, :], xv[:, g * TILES:(g + 1) * TILES, :])\
                    .then_inc(x_rest, 16)

            def stack(g, par, first=False):
                hold(sp, m0_freed, M0_ATT + 4 * g + 3)
                if not first:
                    sp.wait_ge(st_ready, 24 * (g - 1))
                for hg in range(HG):
                    rows = qksplit[32 * hg:32 * hg + 32, par]
                    for r, parts in enumerate((rows[:, 1:3], rows[:, 1:4:2], rows[:, 0:3:2])):
                        sp.dma_start(zc[32 * r:32 * r + 32, par, :, hg, :], parts).then_inc(zc_done, 16)
                sp.wait_ge(zc_done, 192 * (g + 1))
                for r in range(3):
                    for j in range(4):
                        p0 = 32 * r + 8 * j
                        sp.dma_start(zk[p0:p0 + 8, par, :, j, :], zc[p0:p0 + 8, par, 1, :, :])\
                            .then_inc(zk_done, 16)

            sp.wait_ge(zeroed, 2)
            stack(0, 0, first=True)
            stack(1, 1)
            with sp.Fori(0, pairs - 1) as i:
                stack(2 * i + 2, 0)
                stack(2 * i + 3, 1)

            ov = out.rearrange("(t p) d -> p t d", p=P)
            with sp.Fori(0, groups) as g:
                hold(sp, comb_done, done(ALLEXP + E * g + E - 1, D_Y))
                sp.dma_start(ov[:, bass.ds(TILES * g, TILES), :], Xv[:, bass.ds(TILES * g, TILES), :])\
                    .then_inc(out_done, 16)
            sp.wait_ge(out_done, 16 * groups)

        @block.gpsimd
        def _(pool):
            ps = nc.gpsimd
            ps.memset(ident[:, :], 0.0).then_inc(consts, 1)
            ps.memset(causal[:, :, :], 0.0).then_inc(consts, 1)
            ps.iota(rank[:, :, :], pattern=[[0, TILES], [-1, E]], base=E, channel_multiplier=0,
                    allow_small_or_imprecise_dtypes=True).then_inc(consts, 1)
            ps.memset(minus_half[:, :], -0.5).then_inc(consts, 1)
            pool.wait_ge(consts, 4)
            ps.affine_select(out=ident[:, :], in_=ident[:, :], compare_op=ALU.not_equal, fill=1.0, base=0,
                             pattern=[[-1, P]], channel_multiplier=1).then_inc(consts, 1)
            ps.affine_select(out=causal[:, :, :], in_=causal[:, :, :], compare_op=ALU.is_ge, fill=NEG, base=0,
                             pattern=[[0, 4], [-1, P]], channel_multiplier=1).then_inc(consts, 1)
            pool.wait_ge(consts, 6)
            ps.tensor_copy(ident_h[:, :], ident[:, :]).then_inc(consts, 1)
            ps.tensor_copy(ident_b[:, :], ident[:, :]).then_inc(consts, 1)

            def layer_norm(n):
                hold(pool, ln_mean, TILES * (n + 1))
                ps.tensor_scalar(var_eps[:, :], meanvar[:, :, 1], EPS, None, ALU.add).then_inc(eps_added, 1)
                pool.wait_ge(eps_added, done(n))
                ps.tensor_tensor(rstd[:, :], var_eps[:, :], minus_half[:, :], ALU.pow).then_inc(rstd_done, 1)

            def low_part(n, c):
                pool.wait_ge(hi_done, done(n, D_H))
                pool.wait_ge(y_done, freed(n))
                ps.tensor_tensor(hidl[:, c % D_HID, :], prod[:, c % D_H, :], hidh[:, c % D_HID, :],
                                 ALU.subtract).then_inc(lo_done, 1)

            def ffn(phase, n_ln, G, last=False):
                n0 = ALLCHUNKS * (phase // 2) + CHUNKS * G
                for c in range(CHUNKS):
                    if c == 4 and not last:
                        layer_norm(n_ln + G + 1)
                    if c + LAG < CHUNKS or not last:
                        low_part(n0 + c + LAG, (c + LAG) % CHUNKS)

            def ffn_phase(phase):
                n_ln = phase * groups
                layer_norm(n_ln)
                for c in range(LAG):
                    low_part(ALLCHUNKS * (phase // 2) + c, c)
                with pool.Fori(0, pairs - 1) as i:
                    ffn(phase, n_ln, 2 * i)
                    ffn(phase, n_ln, 2 * i + 1)
                ffn(phase, n_ln, groups - 2)
                ffn(phase, n_ln, groups - 1, last=True)

            pool.sem_inc(lo_done, D_H)
            for par in range(2):
                ps.memset(zk[:, par].rearrange("p a b c -> p (a b c)").bitcast(F32), 0.0).then_inc(consts, 1)
                ps.memset(zc[:, par, 0].rearrange("p a b -> p (a b)").bitcast(F32), 0.0).then_inc(consts, 1)
                ps.memset(vaug[:, par], 0.0).then_inc(consts, 1)
            pool.wait_ge(consts, 14)
            for par in range(2):
                ps.memset(vaug[:, par, :, :, DK:DK + 1], 1.0).then_inc(consts, 1)
            pool.wait_ge(consts, 16)
            for par in range(2):
                ps.affine_select(out=zk[96:P, par], in_=zk[96:P, par], compare_op=ALU.not_equal, fill=1.0,
                                 base=0, pattern=[[0, HG], [-1, 4], [0, GTOK]], channel_multiplier=1)\
                    .then_inc(zeroed, 1)
            pool.wait_ge(zeroed, 2)

            ffn_phase(0)

            def clamp(b, q):
                hold(pool, s_reduced, done(12 * b + 11, D_S))
                ps.tensor_scalar(negmax_h[:, q % 2], negmax[:, q % 2], -MLIMIT, MLIMIT, ALU.max, ALU.min)\
                    .then_inc(clamp_done, 1)

            def causal_select(b, hg):
                v = 4 * b + hg
                buf = pt[:, hg]
                hold(pool, exp_done, done(3 * v + 1, D_ST))
                low = buf[:, 0:1024].rearrange("p (h q) -> p h q", q=SEQ)[:, :, 0:P]
                ps.affine_select(out=low, in_=low, compare_op=ALU.is_ge, fill=0.0, base=0,
                                 pattern=[[0, 4], [1, P]], channel_multiplier=-1).then_inc(sel_done, 1)
                hold(pool, exp_done, done(3 * v + 2, D_ST))
                high = buf[:, 1024:1536].rearrange("p (h q) -> p h q", q=P)
                ps.affine_select(out=high, in_=high, compare_op=ALU.is_ge, fill=0.0, base=0,
                                 pattern=[[0, 4], [1, P]], channel_multiplier=-1).then_inc(sel_done, 1)

            def step(b, q, G, scores=True, ln=True):
                for hg in range(HG):
                    causal_select(b, hg)
                    if hg == 1 and q % 2 == 1 and ln:
                        layer_norm(groups + G + 2)
                    if hg == 2 and scores:
                        clamp(b + 1, q + 1)

            layer_norm(groups)
            layer_norm(groups + 1)
            clamp(0, 0)
            step(0, 0, 0)
            with pool.Fori(0, pairs - 1) as i:
                for q in range(1, 5):
                    step(4 * i + q, q, 2 * i + q // 2)
            for q in range(1, 4):
                b = batches - 4 + q
                step(b, q, groups - 2 + q // 2, scores=b + 1 < batches, ln=False)

            ffn_phase(2)

        @block.scalar
        def _(act):
            s = nc.scalar
            act.sem_inc(silu_done, D_H)
            act.sem_inc(hi_done, D_H)
            act.sem_inc(exp_done, D_ST)
            act.sem_inc(o_copied, D_O)

            act.wait_ge(small_loaded, 16)
            s.activation(wsh[:, :], wsmall_f[:, :], ACT.Copy, scale=WSCALE).then_inc(w_hi, 1)

            def x_high(use, par):
                act.wait_ge(m0_ready, done(use))
                s.activation(xh[:, par, :], bank[:, B_M0, :], ACT.Copy).then_inc(m0_hi, 1)

            def chunk(n, c):
                act.wait_ge(h1_ready, done(n))
                act.wait_ge(prod_done, freed(n))
                s.activation(silu[:, c % D_H, :], bank[:, B_H1 + c % 2, :], ACT.Silu, scale=1.0 / WSCALE)\
                    .then_inc(silu_done, 1)
                act.wait_ge(prod_done, done(n, D_H))
                act.wait_ge(y_done, freed(n))
                s.activation(hidh[:, c % D_HID, :], prod[:, c % D_H, :], ACT.Copy).then_inc(hi_done, 1)

            def gate(n):
                act.wait_ge(gate_diff, done(n))
                s.activation(top[:, 5, :], top[:, 4, :], ACT.Tanh, scale=0.5 / WSCALE).then_inc(gate_tanh, 1)

            def ffn(phase, G, par, last=False):
                n0 = ALLCHUNKS * (phase // 2) + CHUNKS * G
                for c in range(CHUNKS):
                    if c + LAG < CHUNKS or not last:
                        chunk(n0 + c + LAG, (c + LAG) % CHUNKS)
                    if c == 9 and not last:
                        x_high(m0_use(phase, G + 1), 1 - par)
                    if c == 14 and not last:
                        gate(groups * (phase // 2) + G + 1)

            def ffn_phase(phase):
                x_high(m0_use(phase, 0), 0)
                if phase == 0:
                    for k in range(4):
                        for n, (wh, cols) in enumerate((
                                (w1h, w1h[:, k * 512:(k + 1) * 512]), (w3h, w3h[:, k * 512:(k + 1) * 512]),
                                (w2h, w2h[:, 4 * k:4 * k + 4, :].rearrange("p a b -> p (a b)")))):
                            act.wait_ge(w_loaded[3 * k + n], 16)
                            s.activation(cols, wstage[:, 3 * k + n, :], ACT.Copy, scale=WSCALE)\
                                .then_inc(w_hi, 1)
                for c in range(LAG):
                    chunk(ALLCHUNKS * (phase // 2) + c, c)
                    if c == 0:
                        gate(groups * (phase // 2))
                with act.Fori(0, pairs - 1) as i:
                    ffn(phase, 2 * i, 0)
                    ffn(phase, 2 * i + 1, 1)
                ffn(phase, groups - 2, 0)
                ffn(phase, groups - 1, 1, last=True)

            ffn_phase(0)

            def q_high(G, par):
                act.wait_ge(m0_ready, done(M0_ATT + 4 * G + 1))
                s.activation(qksplit[:, par, 1, :], bank[:, B_M0, :], ACT.Copy, scale=1.0 / WSCALE)\
                    .then_inc(m0_hi, 1)

            def k_high(G, par):
                act.wait_ge(m0_ready, done(M0_ATT + 4 * G + 2))
                s.activation(qksplit[:, par, 2, :], bank[:, B_M0, :], ACT.Copy, scale=1.0 / WSCALE)\
                    .then_inc(m0_hi, 1)

            def v_copy(G, par):
                act.wait_ge(m0_ready, done(M0_ATT + 4 * G + 3))
                s.activation(vaug[:, par, :, :, 0:DK],
                             bank[:, B_M0, :].rearrange("p (t h d) -> p t h d", t=TILES, d=DK),
                             ACT.Copy, scale=1.0 / WSCALE).then_inc(m0_freed, 1)

            def o_copy(b, q, half):
                act.wait_ge(pv_done, done(4 * b + 2 * half + 1, D_PT))
                s.activation(ot[:, q % 2, 2 * half:2 * half + 2, :].rearrange("p a b -> p (a b)"),
                             bank[:, B_O, :], ACT.Copy).then_inc(o_copied, 1)

            def o_high(u0):
                act.wait_ge(m1_ready, done(u0 + 2))
                s.activation(oh[:, :], bank[:, B_M1, 0:SEQ], ACT.Copy).then_inc(oh_done, 1)

            def step(b, q, G, prev=True, scores=True, qkv=True, ln=True):
                for u in range(12):
                    hg, a = divmod(u, 3)
                    v = 4 * b + hg
                    if a == 0:
                        act.wait_ge(pv_done, freed(v))
                    act.wait_ge(st_ready, done(12 * b + u))
                    s.activation(pt[:, hg, 512 * a:512 * a + 512], bank[:, B_ST + a, :], ACT.Exp,
                                 scale=SM_SCALE).then_inc(exp_done, 1)
                    if u == 3 and prev:
                        o_copy(b - 1, q - 1, 1)
                    if u == 9:
                        if prev:
                            o_high(m1_use(b))
                        o_copy(b, q, 0)
                    if q % 2 == 0 and qkv:
                        par = (q // 2 + 1) % 2
                        if u == 4:
                            q_high(G + 1, par)
                        if u == 6:
                            k_high(G + 1, par)
                        if u == 8:
                            v_copy(G + 1, par)
                    if q % 2 == 1 and ln and u == 10:
                        x_high(m0_use(1, G + 2), (q // 2) % 2)

            x_high(m0_use(1, 0), 0)
            q_high(0, 0)
            k_high(0, 0)
            v_copy(0, 0)
            x_high(m0_use(1, 1), 1)
            step(0, 0, 0, prev=False)
            with act.Fori(0, pairs - 1) as i:
                for q in range(1, 5):
                    step(4 * i + q, q, 2 * i + q // 2)
            for q in range(1, 4):
                b = batches - 4 + q
                step(b, q, groups - 2 + q // 2, qkv=q < 2, ln=False)
            o_copy(batches - 1, 3, 1)
            o_high(M1_TAIL)

            ffn_phase(2)

        @block.vector
        def _(dve):
            v_ = nc.vector
            dve.sem_inc(prod_done, D_H)
            dve.sem_inc(comb_done, D_Y)
            dve.sem_inc(s_reduced, D_S)

            dve.wait_ge(w_hi, 1)
            v_.scalar_tensor_tensor(wsl[:, :], wsmall_f[:, :], WSCALE, wsh[:, :], ALU.mult, ALU.subtract)\
                .then_inc(w_lo, 1)

            def x_tile(t, n=1):
                return X[:, bass.ds(t * D, n * D)]

            def ln_tile(n, t, tile):
                v_.bn_stats(stats[:, t, :], x_tile(tile)).then_inc(ln_stats, 1)
                hold(dve, ln_stats, TILES * n + t + 1)
                v_.bn_aggr(meanvar[:, t, :], stats[:, t, :]).then_inc(ln_mean, 1)

            def normalise(n, t, tile):
                if t == 0:
                    dve.wait_ge(rstd_done, done(n))
                v_.tensor_scalar(xn[:, t, :], x_tile(tile), meanvar[:, t, 0:1], rstd[:, t:t + 1],
                                 ALU.subtract, ALU.mult).then_inc(xn_done, 1)

            def x_low(n_hi, use, par):
                dve.wait_ge(m0_hi, done(n_hi))
                v_.tensor_tensor(xl[:, par, :], bank[:, B_M0, :], xh[:, par, :], ALU.subtract)\
                    .then_inc(m0_freed, 1)

            def hi_use(phase, g):
                if phase == 0:
                    return g
                if phase == 1:
                    return groups + 3 * g
                return 4 * groups + g

            def layer_norm(phase, g, par):
                n = phase * groups + g
                for t in range(TILES):
                    ln_tile(n, t, TILES * g + t)
                for t in range(TILES):
                    normalise(n, t, TILES * g + t)
                x_low(hi_use(phase, g), m0_use(phase, g), par)

            def product(n, c):
                dve.wait_ge(h3_ready, done(n))
                dve.wait_ge(silu_done, done(n, D_H))
                dve.wait_ge(hi_done, freed(n))
                dve.wait_ge(lo_done, freed(n))
                v_.scalar_tensor_tensor(prod[:, c % D_H, :], bank[:, B_H3 + c % 2, :], 1.0 / WSCALE,
                                        silu[:, c % D_H, :], ALU.mult, ALU.mult).then_inc(prod_done, 1)

            def combine(n, e, G, par):
                dve.wait_ge(y_done, done(2 * n + 1, D_HID))
                dve.wait_ge(comb_done, done(n - 1, D_Y))
                for t in range(TILES):
                    last = v_.scalar_tensor_tensor(
                        x_tile(TILES * G + t), bank[:, B_Y + e % 2, t * D:(t + 1) * D],
                        comb[:, par, t, e:e + 1], x_tile(TILES * G + t), ALU.mult, ALU.add)
                last.then_inc(comb_done, 1)

            def bc(col):
                return col.unsqueeze(2).broadcast_to([P, TILES, E])

            def gate_steps(n, par):
                count = [0]

                def link(ins):
                    ins.then_inc(gate_step, 1)
                    count[0] += 1
                    dve.wait_ge(gate_step, GATE_STEPS * n + count[0])

                def first(src, top_row, hot):
                    link(v_.tensor_reduce(top[:, top_row, :], src[:, :, :], AX.X, ALU.max))
                    link(v_.tensor_tensor(score[:, :, :], src[:, :, :], bc(top[:, top_row, :]), ALU.is_equal))
                    link(v_.tensor_tensor(score[:, :, :], score[:, :, :], rank[:, :, :], ALU.mult))
                    link(v_.tensor_reduce(top[:, top_row + 1, :], score[:, :, :], AX.X, ALU.max))
                    link(v_.tensor_tensor(hot[:, :, :], score[:, :, :], bc(top[:, top_row + 1, :]),
                                          ALU.is_equal))

                def part0():
                    dve.wait_ge(gate_ready, done(n))
                    link(v_.tensor_copy(logit[:, :, :].rearrange("p a b -> p (a b)"),
                                        bank[:, B_M1, 0:TILES * E]))
                    first(logit, 0, hot1)

                def part1():
                    link(v_.scalar_tensor_tensor(masked[:, :, :], hot1[:, :, :], NEG, logit[:, :, :],
                                                 ALU.mult, ALU.add))
                    first(masked, 2, hot2)
                    v_.tensor_tensor(top[:, 4, :], top[:, 0, :], top[:, 2, :], ALU.subtract)\
                        .then_inc(gate_diff, 1)

                def part2():
                    dve.wait_ge(gate_tanh, done(n))
                    link(v_.tensor_scalar(top[:, 6, :], top[:, 5, :], 1.0, 0.25 / WSCALE, ALU.add, ALU.mult))
                    link(v_.tensor_scalar(top[:, 7, :], top[:, 5, :], -1.0, -0.25 / WSCALE, ALU.add, ALU.mult))
                    link(v_.tensor_tensor(comb[:, par], hot1[:, :, :], bc(top[:, 6, :]), ALU.mult))
                    link(v_.tensor_tensor(hot2[:, :, :], hot2[:, :, :], bc(top[:, 7, :]), ALU.mult))
                    link(v_.tensor_tensor(comb[:, par], comb[:, par], hot2[:, :, :], ALU.add))
                    assert count[0] == GATE_STEPS

                return part0, part1, part2

            def ffn(phase, G, par, last=False):
                n0 = ALLCHUNKS * (phase // 2) + CHUNKS * G
                e0 = ALLEXP * (phase // 2) + E * G
                nxt = G + 1
                ln = phase * groups + G + 1
                parts = gate_steps(groups * (phase // 2) + G + 1, 1 - par)
                for c in range(CHUNKS):
                    if c + LAG < CHUNKS or not last:
                        product(n0 + c + LAG, (c + LAG) % CHUNKS)
                    if c % 2 == 1:
                        combine(e0 + c // 2, c // 2, G, par)
                    if last:
                        continue
                    if c < TILES:
                        ln_tile(ln, c, TILES * nxt + c)
                    if c in (5, 6):
                        for t in (2 * (c - 5), 2 * (c - 5) + 1):
                            normalise(ln, t, TILES * nxt + t)
                    if c == 9:
                        x_low(hi_use(phase, nxt), m0_use(phase, nxt), 1 - par)
                    if c in (12, 13, 15):
                        parts[(12, 13, 15).index(c)]()

            def ffn_phase(phase):
                layer_norm(phase, 0, 0)
                if phase == 0:
                    for k in range(4):
                        for n, (hi, lo) in enumerate((
                                (w1h[:, k * 512:(k + 1) * 512], w1l[:, k * 512:(k + 1) * 512]),
                                (w3h[:, k * 512:(k + 1) * 512], w3l[:, k * 512:(k + 1) * 512]),
                                (w2h[:, 4 * k:4 * k + 4, :].rearrange("p a b -> p (a b)"),
                                 w2l[:, 4 * k:4 * k + 4, :].rearrange("p a b -> p (a b)")))):
                            dve.wait_ge(w_hi, 2 + 3 * k + n)
                            v_.scalar_tensor_tensor(lo, wstage[:, 3 * k + n, :], WSCALE, hi,
                                                    ALU.mult, ALU.subtract).then_inc(w_lo, 1)
                    dve.wait_ge(consts, 4)
                parts = gate_steps(groups * (phase // 2), 0)
                parts[0]()
                parts[1]()
                product(ALLCHUNKS * (phase // 2), 0)
                parts[2]()
                for c in range(1, LAG):
                    product(ALLCHUNKS * (phase // 2) + c, c)
                if phase == 0:
                    dve.wait_ge(x_rest, 16 * (groups - 1))
                with dve.Fori(0, pairs - 1) as i:
                    ffn(phase, 2 * i, 0)
                    ffn(phase, 2 * i + 1, 1)
                ffn(phase, groups - 2, 0)
                ffn(phase, groups - 1, 1, last=True)

            dve.wait_ge(x_first, 16)
            ffn_phase(0)
            dve.wait_ge(comb_done, done(ALLEXP - 1, D_Y))

            def q_low(G, par):
                dve.wait_ge(m0_hi, done(groups + 3 * G + 1))
                v_.scalar_tensor_tensor(qksplit[:, par, 0, :], bank[:, B_M0, :], 1.0 / WSCALE,
                                        qksplit[:, par, 1, :], ALU.mult, ALU.subtract).then_inc(m0_freed, 1)

            def k_low(G, par):
                dve.wait_ge(m0_hi, done(groups + 3 * G + 2))
                v_.scalar_tensor_tensor(qksplit[:, par, 3, :], bank[:, B_M0, :], 1.0 / WSCALE,
                                        qksplit[:, par, 2, :], ALU.mult, ALU.subtract).then_inc(m0_freed, 1)

            def row_max(b, q, k):
                hg, kind = divmod(k, 3)
                dve.wait_ge(s_ready, done(12 * b + k))
                src = bank[:, B_S + k % 2, :]
                if kind == 0:
                    dst = negmax[:, q % 2, 0, 4 * hg:4 * hg + 4]
                    src = src.rearrange("p (h k) -> p h k", k=P)
                else:
                    h0 = 4 * hg + 2 * (kind - 1)
                    dst = negmax[:, q % 2, 1, h0:h0 + 2]
                    src = src.rearrange("p (h k) -> p h k", k=SEQ)
                v_.tensor_reduce(dst, src, AX.X, ALU.max, negate=True).then_inc(s_reduced, 1)

            def place_max(b, q, use):
                dve.wait_ge(m1_ready, done(use))
                e = q % 2
                v_.tensor_copy(zc[96:100, (q // 2) % 2, 0, :, e * SEQ:(e + 1) * SEQ],
                               bank[96:100, B_M1, :].bitcast(F16).rearrange("p (g q) -> p g q", g=HG))\
                    .then_inc(m1_freed, 1)

            def o_norm(b, u0, qb):
                use = u0 + qb
                view = bank[:, B_M1, :].rearrange("p (h r) -> p h r", r=32)
                dve.wait_ge(m1_ready, done(use))
                v_.reciprocal(rden[:, qb, :], view[:, :, DK]).then_inc(rden_done, 1)
                dve.wait_ge(rden_done, 2 * (b - 1) + qb + 1)
                v_.tensor_tensor(on[:, qb, :].rearrange("p (h d) -> p h d", d=DK), view[:, :, 0:DK],
                                 rden[:, qb, :].unsqueeze(2).broadcast_to([P, HEADS, DK]), ALU.mult)\
                    .then_inc(m1_freed, 1)

            def o_low(b):
                dve.wait_ge(oh_done, b)
                v_.tensor_tensor(ol[:, :], bank[:, B_M1, 0:SEQ], oh[:, :], ALU.subtract).then_inc(m1_freed, 1)

            def x_add(b, u0):
                dve.wait_ge(m1_ready, done(u0 + 3))
                v_.scalar_tensor_tensor(x_tile(2 * (b - 1), 2), bank[:, B_M1, 0:2 * D], 1.0 / WSCALE,
                                        x_tile(2 * (b - 1), 2), ALU.mult, ALU.add).then_inc(m1_freed, 1)

            def step(b, q, G, prev=True, scores=True, qkv=True, ln=True):
                par = (q // 2 + 1) % 2
                for k in range(12):
                    if scores:
                        row_max(b + 1, q + 1, k)
                    if prev and k == 6:
                        o_norm(b, m1_use(b), 0)
                    if prev and k == 9:
                        o_norm(b, m1_use(b), 1)
                    if q % 2 == 0 and qkv and k == 7:
                        q_low(G + 1, par)
                    if q % 2 == 0 and qkv and k == 10:
                        k_low(G + 1, par)
                    if q % 2 == 1 and ln:
                        n = groups + G + 2
                        tile = TILES * (G + 2)
                        if k in (2, 3, 4, 5):
                            ln_tile(n, k - 2, tile + k - 2)
                        if k in (8, 11):
                            for t in (0, 1) if k == 8 else (2, 3):
                                normalise(n, t, tile + t)
                if prev:
                    o_low(b)
                if q % 2 == 1 and ln:
                    x_low(hi_use(1, G + 2), m0_use(1, G + 2), (q // 2) % 2)
                if prev:
                    x_add(b, m1_use(b))
                if scores:
                    place_max(b + 1, q + 1, 5 * b + 1)

            layer_norm(1, 0, 0)
            q_low(0, 0)
            k_low(0, 0)
            layer_norm(1, 1, 1)
            for k in range(12):
                row_max(0, 0, k)
            place_max(0, 0, 0)
            step(0, 0, 0, prev=False)
            with dve.Fori(0, pairs - 1) as i:
                for q in range(1, 5):
                    step(4 * i + q, q, 2 * i + q // 2)
            for q in range(1, 4):
                b = batches - 4 + q
                step(b, q, groups - 2 + q // 2, scores=b + 1 < batches, qkv=q < 2, ln=False)
            o_norm(batches, M1_TAIL, 0)
            o_norm(batches, M1_TAIL, 1)
            o_low(batches)
            x_add(batches, M1_TAIL)
            dve.wait_ge(m1_freed, M1_TAIL + 4)

            ffn_phase(2)

        @block.tensor
        def _(pe):
            t_ = nc.tensor
            pe.sem_inc(y_done, D_HID)
            pe.sem_inc(pv_done, D_PT)

            def x_transpose(n, use):
                pe.wait_ge(xn_done, TILES * (n + 1))
                if not isinstance(use, int) or use > 0:
                    pe.wait_ge(m0_freed, use)
                for t in range(TILES):
                    last = t_.transpose(bank[:, B_M0, t * P:(t + 1) * P], xn[:, t, :], ident[:, :])
                last.then_inc(m0_ready, 1)

            def split_product(dst, ah, al, bh, bl):
                t_.matmul(dst, ah, bh, start=True, stop=False)
                t_.matmul(dst, ah, bl, start=False, stop=False)
                return t_.matmul(dst, al, bh, start=False, stop=True)

            def up(n, c, par, use=None):
                cols = slice(c * P, (c + 1) * P)
                if use is not None:
                    pe.wait_ge(m0_freed, done(use))
                pe.wait_ge(silu_done, freed(n))
                split_product(bank[:, B_H1 + c % 2, :], w1h[:, cols], w1l[:, cols],
                              xh[:, par, :], xl[:, par, :]).then_inc(h1_ready, 1)
                pe.wait_ge(prod_done, freed(n))
                split_product(bank[:, B_H3 + c % 2, :], w3h[:, cols], w3l[:, cols],
                              xh[:, par, :], xl[:, par, :]).then_inc(h3_ready, 1)

            def down(n, ne, c):
                pe.wait_ge(hi_done, done(n, D_H))
                pe.wait_ge(lo_done, done(n, D_H))
                if c % 2 == 0:
                    pe.wait_ge(comb_done, freed(ne))
                for t in range(TILES):
                    toks = slice(t * P, (t + 1) * P)
                    dst = bank[:, B_Y + (c // 2) % 2, toks]
                    hh, hl = hidh[:, c % D_HID, toks], hidl[:, c % D_HID, toks]
                    t_.matmul(dst, hh, w2h[:, c, :], start=c % 2 == 0 and t == 0, stop=False,
                              skip_group_check=True)
                    t_.matmul(dst, hh, w2l[:, c, :], start=False, stop=False, skip_group_check=True)
                    last = t_.matmul(dst, hl, w2h[:, c, :], start=False, stop=c % 2 == 1,
                                     skip_group_check=True)
                last.then_inc(y_done, 1)

            def gate(n, par, use):
                pe.wait_ge(m0_freed, done(use))
                if not isinstance(n, int) or n > 0:
                    pe.wait_ge(gate_step, GATE_STEPS * n)
                g = slice(4 * D, 4 * D + E)
                for t in range(TILES):
                    toks = slice(t * P, (t + 1) * P)
                    dst = bank[:, B_M1, t * E:(t + 1) * E]
                    t_.matmul(dst, xh[:, par, toks], wsh[:, g], start=True, stop=False)
                    t_.matmul(dst, xh[:, par, toks], wsl[:, g], start=False, stop=False)
                    t_.matmul(dst, xl[:, par, toks], wsh[:, g], start=False, stop=False)
                    last = t_.matmul(dst, xl[:, par, toks], wsl[:, g], start=False, stop=True)
                last.then_inc(gate_ready, 1)

            def ffn(phase, G, par, last=False):
                n0 = ALLCHUNKS * (phase // 2) + CHUNKS * G
                e0 = ALLEXP * (phase // 2) + E * G
                nxt = m0_use(phase, G + 1)
                for c in range(CHUNKS):
                    down(n0 + c, e0 + c // 2, c)
                    if c + LAG < CHUNKS:
                        up(n0 + c + LAG, c + LAG, par)
                    elif not last:
                        up(n0 + c + LAG, c + LAG - CHUNKS, 1 - par, nxt if c + LAG == CHUNKS else None)
                    if last:
                        continue
                    if c == 8:
                        x_transpose(phase * groups + G + 1, nxt)
                    if c == 11:
                        gate(groups * (phase // 2) + G + 1, 1 - par, nxt)

            def ffn_phase(phase):
                x_transpose(phase * groups, m0_use(phase, 0))
                if phase == 0:
                    pe.wait_ge(w_lo, 1)
                gate(groups * (phase // 2), 0, m0_use(phase, 0))
                if phase == 0:
                    pe.wait_ge(w_lo, 13)
                for c in range(LAG):
                    up(ALLCHUNKS * (phase // 2) + c, c, 0)
                with pe.Fori(0, pairs - 1) as i:
                    ffn(phase, 2 * i, 0)
                    ffn(phase, 2 * i + 1, 1)
                ffn(phase, groups - 2, 0)
                ffn(phase, groups - 1, 1, last=True)

            pe.wait_ge(consts, 8)
            ffn_phase(0)

            pe.wait_ge(prod_done, done(ALLCHUNKS - 1, D_H))
            pe.wait_ge(comb_done, done(ALLEXP - 1, D_Y))
            WQ, WK, WV, WO = (slice(k * D, (k + 1) * D) for k in range(4))

            def project(G, par, which):
                use = M0_ATT + 4 * G + 1 + which
                pe.wait_ge(m0_freed, use)
                if which < 2:
                    w = (WQ, WK)[which]
                    last = split_product(bank[:, B_M0, :], wsh[:, w], wsl[:, w], xh[:, par, :], xl[:, par, :])
                else:
                    for t in range(TILES):
                        toks = slice(t * P, (t + 1) * P)
                        last = split_product(bank[:, B_M0, toks], xh[:, par, toks], xl[:, par, toks],
                                             wsh[:, WV], wsl[:, WV])
                last.then_inc(m0_ready, 1)

            def scores(b, q, k, G_z=None):
                hg, kind = divmod(k, 3)
                par, e = (q // 2) % 2, q % 2
                if G_z is not None:
                    pe.wait_ge(zc_done, 192 * (G_z + 1))
                    pe.wait_ge(zk_done, 192 * (G_z + 1))
                pe.wait_ge(s_reduced, freed(12 * b + k))
                dst = bank[:, B_S + k % 2, :]
                q0 = e * SEQ + (0 if kind == 0 else P)
                qs = zc[0:96, par, 0, hg, q0:q0 + P]
                if kind == 0:
                    t_.matmul(dst, qs, zk[0:96, par, hg, :, e * SEQ:e * SEQ + P], start=True, stop=False)
                    t_.matmul(dst, ident_b[:, :], causal[:, :, :], start=False, stop=True)\
                        .then_inc(s_ready, 1)
                else:
                    j = 2 * (kind - 1)
                    t_.matmul(dst, qs, zk[0:96, par, hg, j:j + 2, e * SEQ:(e + 1) * SEQ],
                              start=True, stop=False, skip_group_check=True)
                    t_.matmul(dst.rearrange("p (h k) -> p h k", k=SEQ)[:, :, P:SEQ], ident_b[:, :],
                              causal[:, 0:2, :], start=False, stop=True, skip_group_check=True)\
                        .then_inc(s_ready, 1)

            def max_transpose(b, q, use):
                pe.wait_ge(clamp_done, done(b))
                if not isinstance(use, int) or use > 0:
                    pe.wait_ge(m1_freed, use)
                dst = bank[96:100, B_M1, :].bitcast(F16)
                for qb in range(2):
                    for hg in range(HG):
                        last = t_.transpose(dst[:, hg * SEQ + qb * P:hg * SEQ + qb * P + P],
                                            negmax_h[:, q % 2, qb, 4 * hg:4 * hg + 4], ident_h[:, :])
                last.then_inc(m1_ready, 1)

            def scores_t(b, q, u):
                hg, a = divmod(u, 3)
                par, e = (q // 2) % 2, q % 2
                if u == 0:
                    pe.wait_ge(m1_freed, 1 if isinstance(b, int) and b == 0 else m1_use(b))
                pe.wait_ge(exp_done, freed(12 * b + u))
                dst = bank[:, B_ST + a, :]
                k0 = e * SEQ + (0 if a < 2 else P)
                heads = (0, 1) if a == 0 else (2, 3) if a == 1 else (0, 1, 2, 3)
                nq = SEQ if a < 2 else P
                for m, j in enumerate(heads):
                    last = t_.matmul(dst[:, m * nq:(m + 1) * nq], zk[:, par, hg, j, k0:k0 + P],
                                     zc[:, par, 0, hg, (e + 1) * SEQ - nq:(e + 1) * SEQ],
                                     start=True, stop=True)
                last.then_inc(st_ready, 1)

            def values(b, q, hg):
                v = 4 * b + hg
                par, e = (q // 2) % 2, q % 2
                pe.wait_ge(sel_done, 2 * v + 2)
                if hg % 2 == 0:
                    pe.wait_ge(o_copied, freed(2 * b + hg // 2))
                c0 = (hg % 2) * SEQ
                buf = pt[:, hg]
                for j in range(4):
                    t_.matmul(bank[32 * j:32 * j + 32, B_O, c0:c0 + SEQ], vaug[:, par, 2 * e, 4 * hg + j, :],
                              buf[:, j * SEQ:(j + 1) * SEQ], start=True, stop=False, skip_group_check=True)
                for j in range(4):
                    last = t_.matmul(bank[32 * j:32 * j + 32, B_O, c0 + P:c0 + SEQ],
                                     vaug[:, par, 2 * e + 1, 4 * hg + j, :],
                                     buf[:, 1024 + j * P:1024 + (j + 1) * P], start=False, stop=True,
                                     skip_group_check=True)
                last.then_inc(pv_done, 1)

            def o_back(b, q, u0, qb):
                use = u0 + qb
                pe.wait_ge(o_copied, done(2 * (b - 1) + 1, D_O))
                pe.wait_ge(m1_freed, use)
                for hg in range(HG):
                    last = t_.transpose(bank[:, B_M1, hg * P:(hg + 1) * P],
                                        ot[:, (q - 1) % 2, hg, qb * P:(qb + 1) * P], ident[:, :])
                last.then_inc(m1_ready, 1)

            def o_transpose(u0):
                use = u0 + 2
                pe.wait_ge(m1_freed, use)
                for qb in range(2):
                    last = t_.transpose(bank[:, B_M1, qb * P:(qb + 1) * P], on[:, qb, :], ident[:, :])
                last.then_inc(m1_ready, 1)

            def o_project(u0):
                use = u0 + 3
                pe.wait_ge(m1_freed, use)
                for qb in range(2):
                    toks = slice(qb * P, (qb + 1) * P)
                    last = split_product(bank[:, B_M1, toks], oh[:, toks], ol[:, toks], wsh[:, WO], wsl[:, WO])
                last.then_inc(m1_ready, 1)

            def step(b, q, G, prev=True, more=True, qkv=True, ln=True):
                issued = 0
                for u in range(12):
                    quota = min(12, -(-(u + 1) * 12 // 9))
                    while more and issued < quota:
                        scores(b + 1, q + 1, issued, (G + 1 if q % 2 == 1 else None) if issued == 0 else None)
                        issued += 1
                    scores_t(b, q, u)
                    if u == 2 and prev:
                        values(b - 1, q - 1, 3)
                    if u == 3:
                        if prev:
                            o_back(b, q, m1_use(b), 0)
                        if q % 2 == 0 and qkv:
                            project(G + 1, (q // 2 + 1) % 2, 0)
                    if u == 5:
                        values(b, q, 0)
                        if prev:
                            o_back(b, q, m1_use(b), 1)
                        if q % 2 == 0 and qkv:
                            project(G + 1, (q // 2 + 1) % 2, 1)
                    if u == 7:
                        if prev:
                            o_transpose(m1_use(b))
                        if q % 2 == 0 and qkv:
                            project(G + 1, (q // 2 + 1) % 2, 2)
                    if u == 8:
                        values(b, q, 1)
                    if u == 9 and q % 2 == 1 and ln:
                        x_transpose(groups + G + 2, m0_use(1, G + 2))
                    if u == 10 and prev:
                        o_project(m1_use(b))
                    if u == 11:
                        values(b, q, 2)
                        if more:
                            max_transpose(b + 1, q + 1, 5 * b + 1)

            x_transpose(groups, m0_use(1, 0))
            for which in range(3):
                project(0, 0, which)
            x_transpose(groups + 1, m0_use(1, 1))
            pe.wait_ge(consts, 16)
            for k in range(12):
                scores(0, 0, k, 0 if k == 0 else None)
            max_transpose(0, 0, 0)
            step(0, 0, 0, prev=False)
            with pe.Fori(0, pairs - 1) as i:
                for q in range(1, 5):
                    step(4 * i + q, q, 2 * i + q // 2)
            for q in range(1, 4):
                b = batches - 4 + q
                step(b, q, groups - 2 + q // 2, more=b + 1 < batches, qkv=q < 2, ln=False)
            values(batches - 1, 3, 3)
            o_back(batches, 0, M1_TAIL, 0)
            o_back(batches, 0, M1_TAIL, 1)
            o_transpose(M1_TAIL)
            o_project(M1_TAIL)

            pe.wait_ge(exp_done, done(12 * batches - 1, D_ST))
            pe.wait_ge(m1_freed, M1_TAIL + 4)
            ffn_phase(2)


_INS = ("x_in", "w_up1", "w_up3", "w_down", "w_small")


def kernel(L0_attn_x, L0_attn_WQ, L0_attn_WK, L0_attn_WV, L0_attn_WO, L0_ffn_gate_w, L0_ffn_w1,
           L0_ffn_w2, L0_ffn_w3):
    import concourse.bacc as bacc
    from concourse.bass_utils import run_bass_kernel_spmd

    x = np.asarray(L0_attn_x)
    batches, seq, d = x.shape
    assert (seq, d) == (SEQ, D)
    w1 = np.asarray(L0_ffn_w1).reshape(E * HID, D).T
    w3 = np.asarray(L0_ffn_w3).reshape(E * HID, D).T
    w2 = np.asarray(L0_ffn_w2).transpose(0, 2, 1).reshape(CHUNKS, P, D).transpose(1, 0, 2).reshape(P, -1)
    small = np.concatenate([np.asarray(w) for w in (L0_attn_WQ, L0_attn_WK, L0_attn_WV, L0_attn_WO)]
                           + [np.asarray(L0_ffn_gate_w).T], axis=1)
    arrays = dict(zip(_INS, (np.ascontiguousarray(a) for a in (x.reshape(-1, D), w1, w3, w2, small))))

    nc = bacc.Bacc("TRN2", target_bir_lowering=False, num_devices=1)
    args = [nc.dram_tensor(n, arrays[n].shape, F32, kind="ExternalInput").ap() for n in _INS]
    out = nc.dram_tensor("out", (batches * SEQ, D), F32, kind="ExternalOutput").ap()
    build_macaron(nc, *args, out, batches)
    r = run_bass_kernel_spmd(nc, [arrays], core_ids=[0])
    return r.results[0]["out"].reshape(batches, SEQ, D)
```

```python
from contextlib import ExitStack

import numpy as np

import concourse.bass as bass
from concourse import mybir

F32 = mybir.dt.float32
F16 = mybir.dt.float16
BF16 = mybir.dt.bfloat16
I32 = mybir.dt.int32
ALU = mybir.AluOpType
ACT = mybir.ActivationFunctionType
AX = mybir.AxisListType

P = 128
D = 128
SEQ = 256
HEADS, DK = 16, 8
E, HID = 8, 256
TILES = 4
GTOK = TILES * P
CHUNKS = E * HID // P
LAG = 3
HG = 4
WSCALE = 256.0
EPS = 1e-5
NEG = -1.0e30
MLIMIT = 60000.0
SM_SCALE = DK ** -0.5

SLOTS = 256
HT = 16
HGROUPS = HT // TILES
HTOK = HT * P
NT = (2 * HTOK + E * (SLOTS - 1)) // SLOTS
ETILES = HTOK // SLOTS
LOOPS = (NT - LAG) // 4
assert NT == 4 * LOOPS + LAG
ROUTE_STEPS = 35
ROUTE_USES = 2 * HGROUPS + 1

D_H = 2
D_HID = 4
D_Y = 2
D_IO = 4
D_YG = 3
D_S = 2
D_ST = 3
D_PT = 4
D_O = 1


def freed(n):
    return n + 1


def done(n, depth=0):
    return n + 1 + depth


def build_macaron(nc, x_in, w_up1, w_up3, w_down, w_small, out, batches):
    groups = batches * SEQ // GTOK
    pairs = groups // 2
    assert groups == 2 * pairs and pairs >= 3 and batches == 4 * pairs and groups == 2 * HGROUPS
    rows = NT * SLOTS
    sorted_x = [nc.dram_tensor(f"sorted_x{k}", (rows, 2 * D), F16, kind="Internal").ap() for k in range(2)]
    sorted_y = [nc.dram_tensor(f"sorted_y{k}", (rows, D), F32, kind="Internal").ap() for k in range(2)]
    ctx = ExitStack()
    with ctx:
        def sb(name, shape, dt):
            return ctx.enter_context(nc.sbuf_tensor(name, shape, dt))

        def sem(name):
            return ctx.enter_context(nc.semaphore(name))

        X = sb("X", [P, groups * TILES * D], F32)
        w1h = sb("w1h", [P, E * HID], F16)
        w1l = sb("w1l", [P, E * HID], F16)
        w3h = sb("w3h", [P, E * HID], F16)
        w3l = sb("w3l", [P, E * HID], F16)
        w2h = sb("w2h", [P, CHUNKS * D], F16)
        w2l = sb("w2l", [P, CHUNKS * D], F16)
        NSMALL = 4 * D + E
        wsh = sb("wsh", [P, NSMALL], F16)
        wsl = sb("wsl", [P, NSMALL], F16)
        wsmall_f = sb("wsmall_f", [P, NSMALL], F32)
        ident = sb("ident", [P, P], F32)
        ident_h = sb("ident_h", [P, P], F16)
        ident_b = sb("ident_b", [P, P], BF16)
        causal = sb("causal", [P, 4, P], BF16)
        rank = sb("rank", [P, HT, E], F32)
        earlier = sb("earlier", [P, P], BF16)
        ones_b = sb("ones_b", [P, P], BF16)
        zeros = sb("zeros", [P, 2 * D], F16)
        bounds = sb("bounds", [P, E, ETILES], F32)
        before = sb("before", [P, E, E], F32)
        tile_no = sb("tile_no", [P, NT + 1, E - 1], F32)
        stats = sb("stats", [P, TILES, 6], F32)
        meanvar = sb("meanvar", [P, TILES, 2], F32)
        var_eps = sb("var_eps", [P, TILES], F32)
        minus_half = sb("minus_half", [P, TILES], F32)
        rstd = sb("rstd", [P, TILES], F32)
        xn = sb("xn", [P, TILES, D], F32)
        xh = sb("xh", [P, 2, GTOK], F16)
        xl = sb("xl", [P, 2, GTOK], F16)
        xs = sb("xs", [P, 2, HT, 2 * D], F16)
        xth = sb("xth", [P, 2, GTOK], F16)
        logit = sb("logit", [P, HT, E], F32)
        masked = sb("masked", [P, HT, E], F32)
        score = sb("score", [P, HT, E], F32)
        hot1 = sb("hot1", [P, HT, E], F32)
        hot2 = sb("hot2", [P, HT, E], F32)
        top = sb("top", [P, 6, HT], F32)
        chosen = sb("chosen", [P, HT + 1, E], BF16)
        over = sb("over", [P, E, ETILES], F32)
        ntiles = sb("ntiles", [P, E], F32)
        shares = sb("shares", [P, E, E], F32)
        start = sb("start", [P, E], F32)
        passed = sb("passed", [P, NT + 1, E - 1], F32)
        expert = sb("expert", [P, NT + 1], F32)
        woffset = sb("woffset", [P, 2, NT + 1], I32)
        place = sb("place", [P, HT, E], F32)
        rowf = sb("rowf", [P, 2, HT], F32)
        row = sb("row", [P, 2, 2, HT], I32)
        weight = sb("weight", [P, 2, 2, HT], F32)
        yg = sb("yg", [P, D_YG, 2, D], F32)
        qksplit = sb("qksplit", [P, 2, 4, GTOK], F16)
        zc = sb("zc", [P, 2, 2, HG, GTOK], F16)
        zk_flat = sb("zk_flat", [P, 2 * HG * 4 * GTOK], F16)
        zk = zk_flat[:, :].rearrange("p (a g j n) -> p a g j n", a=2, g=HG, j=4)
        taken = [0]

        def part_of(n, shape, dt=F16):
            size = n * int(np.prod(shape)) * (2 if dt is F32 else 1)
            cols = zk_flat[:, taken[0]:taken[0] + size]
            taken[0] += size
            assert taken[0] <= 2 * HG * 4 * GTOK
            if dt is F32:
                cols = cols.bitcast(F32)
            if len(shape) == 1:
                return cols.rearrange("p (n a) -> p n a", n=n)
            return cols.rearrange("p (n a b) -> p n a b", n=n, a=shape[0])

        silu = part_of(D_H, [2 * SLOTS], F32)
        prod = part_of(D_H, [2 * SLOTS], F32)
        yb = part_of(D_IO, [2, D], F32)
        hidh = part_of(D_HID, [2 * SLOTS])
        hidl = part_of(D_HID, [2 * SLOTS])
        xt = part_of(2, [2, SLOTS])
        xg = part_of(D_IO, [2, 2 * D])
        diag4 = sb("diag4", [P, 4, 4], F32)
        diag = sb("diag", [P, 4], F32)
        vaug = sb("vaug", [P, 2, TILES, HEADS, 32], F32)
        negmax = sb("negmax", [P, 2, 2, HEADS], F32)
        negmax_h = sb("negmax_h", [P, 2, 2, HEADS], F16)
        pt = sb("pt", [P, D_PT, 3 * 512], F32)
        ot = sb("ot", [P, 2, HG, SEQ], F32)
        rden = sb("rden", [P, 2, HEADS], F32)
        on = sb("on", [P, 2, D], F32)
        oh = sb("oh", [P, SEQ], F16)
        ol = sb("ol", [P, SEQ], F16)
        wstage = pt[:, :, :].rearrange("p a b -> p (a b)").rearrange("p (k n) -> p k n", n=512)

        bank = ctx.enter_context(nc.psum_tensor("bank", [P, 8, 512], F32))
        B_H1, B_H3, B_Y, B_T = 0, 2, 4, 6
        B_S, B_ST, B_O = 0, 2, 5
        B_M0, B_M1 = 6, 7

        def t_bank(q):
            return bank[:, B_T + q % 2, 0:SLOTS].bitcast(F16)

        x_first = sem("x_first")
        x_rest = sem("x_rest")
        small_loaded = sem("small_loaded")
        w_loaded = [sem(f"w_loaded{k}") for k in range(12)]
        w_hi = sem("w_hi")
        w_lo = sem("w_lo")
        consts = sem("consts")
        ln_stats = sem("ln_stats")
        ln_mean = sem("ln_mean")
        eps_added = sem("eps_added")
        rstd_done = sem("rstd_done")
        xn_done = sem("xn_done")
        m0_ready = sem("m0_ready")
        m0_hi = sem("m0_hi")
        m0_freed = sem("m0_freed")
        h1_ready = sem("h1_ready")
        h3_ready = sem("h3_ready")
        silu_done = sem("silu_done")
        prod_done = sem("prod_done")
        hi_done = sem("hi_done")
        lo_even = sem("lo_even")
        lo_odd = sem("lo_odd")
        y_ready = sem("y_ready")
        y_copied = sem("y_copied")
        t_ready = sem("t_ready")
        t_copied = sem("t_copied")
        xs_hi = sem("xs_hi")
        xs_lo = sem("xs_lo")
        gate_step = sem("gate_step")
        gate_diff = sem("gate_diff")
        gate_tanh = sem("gate_tanh")
        hot_done = sem("hot_done")
        rows_done = sem("rows_done")
        tiles_done = sem("tiles_done")
        zeroed = sem("zeroed")
        scattered = sem("scattered")
        xg_loaded = [sem(f"xg_loaded{k}") for k in range(D_IO)]
        y_stored = [sem(f"y_stored{k}") for k in range(D_IO)]
        gathered = [sem(f"gathered{k}") for k in range(D_YG)]
        x_sum = sem("x_sum")
        s_ready = sem("s_ready")
        s_reduced = sem("s_reduced")
        clamp_done = sem("clamp_done")
        m_placed = sem("m_placed")
        st_ready = sem("st_ready")
        exp_done = sem("exp_done")
        sel_done = sem("sel_done")
        pv_done = sem("pv_done")
        o_copied = sem("o_copied")
        m1_ready = sem("m1_ready")
        m1_freed = sem("m1_freed")
        oh_done = sem("oh_done")
        ol_done = sem("ol_done")
        rden_done = sem("rden_done")
        on_done = sem("on_done")
        x_attn = sem("x_attn")
        zc_done = sem("zc_done")
        zk_done = sem("zk_done")
        vaug_set = sem("vaug_set")
        diag_step = sem("diag_step")
        diag_done = sem("diag_done")
        out_done = sem("out_done")

        held = sem("held")

        def hold(eng, what, value):
            eng.wait_ge(what, value)
            eng.sem_inc(held, 1)

        def no_use(eng, use, count):
            if count is m1_freed:
                eng.wait_ge(m1_freed, use)
                eng.wait_ge(m1_ready, use + 1)
            eng.sem_inc(count, 1)

        def unit_count(s, k):
            return s * (5 + (1 if k == 0 else 0))

        CONSTS = 21
        block = ctx.enter_context(nc.Block())

        M0_ATT = 2 * ROUTE_USES

        def m0_route(s):
            return ROUTE_USES * s + (4 * groups if s >= 2 else 0)

        def m0_use(g):
            return M0_ATT + 4 * g

        def io_use(s, q, j):
            return s * (LOOPS + (1 if q < LAG else 0)) + j

        def lo_use(s, q, j):
            return s * (NT // 2 + (1 - q % 2)) + 2 * j + q // 2

        def units(j, u):
            return 3 * j + u

        PREV = NT - 1

        def m1_use(b):
            return 5 * b - 2

        def max_use(b):
            return m1_use(b) + 3

        M1_TAIL = m1_use(batches)

        @block.sync
        def _(sp):
            xv = x_in.rearrange("(t p) d -> p t d", p=P)
            Xv = X[:, :].rearrange("p (t d) -> p t d", d=D)
            sp.dma_start(Xv[:, 0:TILES, :], xv[:, 0:TILES, :]).then_inc(x_first, 16)
            sp.dma_start(wsmall_f[:, :], w_small).then_inc(small_loaded, 16)
            for g in range(1, groups):
                sp.dma_start(Xv[:, g * TILES:(g + 1) * TILES, :], xv[:, g * TILES:(g + 1) * TILES, :])\
                    .then_inc(x_rest, 16)
            sp.wait_ge(consts, 1)
            for k in range(2):
                sp.dma_start(sorted_x[k].rearrange("(t p) d -> p t d", p=P),
                             zeros[:, :].unsqueeze(1).broadcast_to([P, rows // P, 2 * D])).then_inc(zeroed, 16)
                if k == 0:
                    for m in range(4):
                        for n, w in enumerate((w_up1, w_up3, w_down)):
                            sp.dma_start(wstage[:, 3 * m + n, :], w[:, m * 512:(m + 1) * 512])\
                                .then_inc(w_loaded[3 * m + n], 16)

            def load(s, q, j):
                i = 4 * j + q
                if not isinstance(j, int) or j > 0:
                    hold(sp, t_ready, NT * s + i - D_IO + 1)
                sp.dma_start(xg[:, q], sorted_x[s % 2].rearrange("(t u p) d -> p t u d", p=P, u=2)
                             [:, bass.ds(i, 1)].rearrange("p a u d -> p (a u) d")).then_inc(xg_loaded[q], 16)

            def experts(s):
                sp.wait_ge(scattered, 16 * 2 * HT * (s + 1))
                if s > 0:
                    sp.wait_ge(t_ready, NT * s)
                if s == 2:
                    sp.wait_ge(st_ready, done(12 * batches - 1))
                if s >= 2:
                    for k in range(D_YG):
                        sp.wait_ge(gathered[k], 32 * unit_count(s - 1, k))
                for q in range(LAG):
                    load(s, q, 0)
                load(s, LAG, 0)
                with sp.Fori(1, LOOPS) as j:
                    for q in range(D_IO):
                        load(s, q, j)
                for q in range(LAG):
                    load(s, q, LOOPS)

            experts(0)
            experts(1)

            sp.wait_ge(consts, CONSTS)

            def stack(g, par, first=False):
                hold(sp, m0_freed, m0_use(g) + 3)
                if not first:
                    sp.wait_ge(st_ready, 24 * (g - 1))
                for hg in range(HG):
                    rows = qksplit[32 * hg:32 * hg + 32, par]
                    for r, parts in enumerate((rows[:, 1:3], rows[:, 1:4:2], rows[:, 0:3:2])):
                        sp.dma_start(zc[32 * r:32 * r + 32, par, :, hg, :], parts).then_inc(zc_done, 16)

            stack(0, 0, first=True)
            stack(1, 1)
            with sp.Fori(0, pairs - 1) as i:
                stack(2 * i + 2, 0)
                stack(2 * i + 3, 1)

            experts(2)
            experts(3)
            ov = out.rearrange("(t p) d -> p t d", p=P)
            with sp.Fori(0, groups) as g:
                hold(sp, x_sum, 2 * 2 * groups * TILES - 2 * TILES * (groups - 1) + 2 * TILES * g)
                sp.dma_start(ov[:, bass.ds(TILES * g, TILES), :], Xv[:, bass.ds(TILES * g, TILES), :])\
                    .then_inc(out_done, 16)
            sp.wait_ge(out_done, 16 * groups)

        @block.gpsimd
        def _(pool):
            ps = nc.gpsimd
            pool.sem_inc(lo_even, 1)
            ps.memset(zeros[:, :], 0.0).then_inc(consts, 1)
            ps.memset(minus_half[:, :], -0.5).then_inc(consts, 1)
            ps.memset(ident[:, :], 0.0).then_inc(consts, 1)
            pool.wait_ge(consts, 3)
            ps.affine_select(out=ident[:, :], in_=ident[:, :], compare_op=ALU.not_equal, fill=1.0, base=0,
                             pattern=[[-1, P]], channel_multiplier=1).then_inc(consts, 1)
            pool.wait_ge(consts, 4)
            ps.tensor_copy(ident_h[:, :], ident[:, :]).then_inc(consts, 1)
            ps.tensor_copy(ident_b[:, :], ident[:, :]).then_inc(consts, 1)

            def routing_constants():
                ps.iota(rank[:, :, :], pattern=[[0, HT], [-1, E]], base=E, channel_multiplier=0,
                        allow_small_or_imprecise_dtypes=True).then_inc(consts, 1)
                ps.memset(ones_b[:, :], 1.0).then_inc(consts, 1)
                ps.memset(earlier[:, :], 1.0).then_inc(consts, 1)
                ps.memset(chosen[:, HT, :], 0.0).then_inc(consts, 1)
                ps.memset(before[:, :, :], 1.0).then_inc(consts, 1)
                ps.iota(bounds[:, :, :], pattern=[[0, E], [SLOTS, ETILES]], base=0, channel_multiplier=0,
                        allow_small_or_imprecise_dtypes=True).then_inc(consts, 1)
                ps.iota(tile_no[:, :, :], pattern=[[1, NT + 1], [0, E - 1]], base=0, channel_multiplier=0,
                        allow_small_or_imprecise_dtypes=True).then_inc(consts, 1)
                ps.memset(causal[:, :, :], 0.0).then_inc(consts, 1)
                pool.wait_ge(consts, 14)
                ps.affine_select(out=earlier[:, :], in_=earlier[:, :], compare_op=ALU.is_ge, fill=0.0,
                                 base=-1, pattern=[[1, P]], channel_multiplier=-1).then_inc(consts, 1)
                ps.affine_select(out=before[:, :, :], in_=before[:, :, :], compare_op=ALU.is_ge, fill=0.0,
                                 base=-1, pattern=[[1, E], [-1, E]], channel_multiplier=0).then_inc(consts, 1)
                pool.wait_ge(consts, 16)
                ps.affine_select(out=causal[:, :, :], in_=causal[:, :, :], compare_op=ALU.is_ge, fill=NEG,
                                 base=0, pattern=[[0, 4], [-1, P]], channel_multiplier=1).then_inc(consts, 1)

            def attention_constants():
                for par in range(2):
                    ps.memset(zc[:, par, 0].rearrange("p a b -> p (a b)").bitcast(F32), 0.0)\
                        .then_inc(consts, 1)
                    ps.memset(zc[:, par, 1], 1.0).then_inc(consts, 1)
                ps.memset(vaug[:, :], 0.0).then_inc(vaug_set, 1)
                pool.wait_ge(vaug_set, 1)
                ps.memset(vaug[:, :, :, :, DK:DK + 1], 1.0).then_inc(vaug_set, 1)
                ps.memset(diag4[:, :, :], 1.0).then_inc(diag_step, 1)
                pool.wait_ge(diag_step, 1)
                ps.memset(diag4[:, 3, :], 0.0).then_inc(diag_step, 1)
                part = diag4[:, 0:3, :]
                pool.wait_ge(diag_step, 2)
                ps.affine_select(out=part, in_=part, compare_op=ALU.is_ge, fill=0.0, base=0,
                                 pattern=[[-32, 3], [-DK, 4]], channel_multiplier=1).then_inc(diag_step, 1)
                pool.wait_ge(diag_step, 3)
                ps.affine_select(out=part, in_=part, compare_op=ALU.is_ge, fill=0.0, base=DK - 1,
                                 pattern=[[32, 3], [DK, 4]], channel_multiplier=-1).then_inc(diag_step, 1)
                ps.affine_select(out=diag4[:, 3, :], in_=diag4[:, 3, :], compare_op=ALU.not_equal, fill=1.0,
                                 base=-96, pattern=[[-1, 4]], channel_multiplier=1).then_inc(diag_step, 1)

            def layer_norm(n):
                hold(pool, ln_mean, TILES * (n + 1))
                ps.tensor_scalar(var_eps[:, :], meanvar[:, :, 1], EPS, None, ALU.add).then_inc(eps_added, 1)
                pool.wait_ge(eps_added, done(n))
                ps.tensor_tensor(rstd[:, :], var_eps[:, :], minus_half[:, :], ALU.pow).then_inc(rstd_done, 1)

            def low_part(s, i):
                n = NT * s + i
                pool.wait_ge(hi_done, done(n, D_H))
                pool.wait_ge(y_ready, freed(n))
                ps.tensor_tensor(hidl[:, i % D_HID], prod[:, i % D_H], hidh[:, i % D_HID],
                                 ALU.subtract).then_inc(lo_even, 1)

            def scatter(s, t):
                if t == 0:
                    pool.wait_ge(rows_done, s + 1)
                    pool.wait_ge(xs_lo, HGROUPS * (s + 1))
                    if s == 0:
                        pool.wait_ge(zeroed, 32)
                    if s >= 2:
                        for q in range(D_IO):
                            pool.wait_ge(xg_loaded[q], 16 * io_use(s - 1, q, 0))
                for k in range(2):
                    ps.indirect_dma_start(
                        out=sorted_x[s % 2],
                        out_offset=bass.IndirectOffsetOnAxis(ap=row[:, s % 2, k, t:t + 1], axis=0),
                        in_=xs[:, s % 2, t, :], in_offset=None).then_inc(scattered, 16)

            def gather(s, t):
                if t == 0:
                    for q in range(D_IO):
                        pool.wait_ge(y_stored[q], 16 + 16 * io_use(s + 1, q, 0))
                before_this = HT * s + t - D_YG
                if t >= D_YG:
                    pool.wait_ge(x_sum, 2 * (before_this + 1))
                elif s > 0:
                    pool.wait_ge(x_sum, 2 * HT * s)
                for k in range(2):
                    ps.indirect_dma_start(
                        out=yg[:, t % D_YG, k, :], out_offset=None, in_=sorted_y[s % 2],
                        in_offset=bass.IndirectOffsetOnAxis(ap=row[:, s % 2, k, t:t + 1], axis=0))\
                        .then_inc(gathered[t % D_YG], 16)

            def experts(s, side, other):
                t = 0
                for i in range(NT):
                    if i % 2 == 0:
                        low_part(s, i)
                    if t < HT and i >= LAG - 2 and (i - LAG + 2) % 4 != 3:
                        side(other, t)
                        t += 1
                assert t == HT

            def expert_phase(phase):
                s = 2 * phase
                n = 2 * phase * groups
                for g in range(HGROUPS):
                    layer_norm(n + g)
                    if phase == 0 and g == 0:
                        routing_constants()
                if phase == 0:
                    attention_constants()
                for t in range(HT):
                    scatter(s, t)
                    if t % 4 == 1:
                        layer_norm(n + HGROUPS + t // 4)
                experts(s, scatter, s + 1)
                experts(s + 1, gather, s)
                for t in range(HT):
                    gather(s + 1, t)

            expert_phase(0)

            def clamp(b, q):
                hold(pool, s_reduced, done(12 * b + 11, D_S))
                ps.tensor_scalar(negmax_h[:, q % 2], negmax[:, q % 2], -MLIMIT, MLIMIT, ALU.max, ALU.min)\
                    .then_inc(clamp_done, 1)

            def causal_select(b, hg):
                v = 4 * b + hg
                buf = pt[:, hg]
                hold(pool, exp_done, done(3 * v + 1, D_ST))
                low = buf[:, 0:1024].rearrange("p (h q) -> p h q", q=SEQ)[:, :, 0:P]
                ps.affine_select(out=low, in_=low, compare_op=ALU.is_ge, fill=0.0, base=0,
                                 pattern=[[0, 4], [1, P]], channel_multiplier=-1).then_inc(sel_done, 1)
                hold(pool, exp_done, done(3 * v + 2, D_ST))
                high = buf[:, 1024:1536].rearrange("p (h q) -> p h q", q=P)
                ps.affine_select(out=high, in_=high, compare_op=ALU.is_ge, fill=0.0, base=0,
                                 pattern=[[0, 4], [1, P]], channel_multiplier=-1).then_inc(sel_done, 1)

            def step(b, q, G, scores=True, ln=True):
                for hg in range(HG):
                    causal_select(b, hg)
                    if hg == 1 and q % 2 == 1 and ln:
                        layer_norm(groups + G + 2)
                    if hg == 2 and scores:
                        clamp(b + 1, q + 1)

            layer_norm(groups)
            layer_norm(groups + 1)
            clamp(0, 0)
            step(0, 0, 0)
            with pool.Fori(0, pairs - 1) as i:
                for q in range(1, 5):
                    step(4 * i + q, q, 2 * i + q // 2)
            for q in range(1, 4):
                b = batches - 4 + q
                step(b, q, groups - 2 + q // 2, scores=b + 1 < batches, ln=False)

            expert_phase(1)

        @block.scalar
        def _(act):
            s_ = nc.scalar
            act.sem_inc(silu_done, D_H)
            act.sem_inc(hi_done, D_H)
            act.sem_inc(y_copied, D_Y)
            for q in range(D_IO):
                act.sem_inc(y_stored[q], 16)
            act.sem_inc(exp_done, D_ST)
            act.sem_inc(o_copied, D_O)

            act.wait_ge(small_loaded, 16)
            s_.activation(wsh[:, :], wsmall_f[:, :], ACT.Copy, scale=WSCALE).then_inc(w_hi, 1)

            def x_high(use, par):
                act.wait_ge(m0_ready, done(use))
                s_.activation(xh[:, par, :], bank[:, B_M0, :], ACT.Copy).then_inc(m0_hi, 1)

            def parts_high(s, g):
                n = HGROUPS * s + g
                act.wait_ge(xn_done, TILES * (n + (groups if s >= 2 else 0) + 1))
                s_.activation(xs[:, s % 2, bass.ds(TILES * g, TILES), 0:D], xn[:, :, :], ACT.Copy)\
                    .then_inc(xs_hi, 1)
                act.wait_ge(m0_ready, done(m0_route(s) + 2 * g))
                s_.activation(xth[:, :, :].rearrange("p a b -> p (a b)"), bank[:, B_M0, :].bitcast(F16),
                              ACT.Copy).then_inc(m0_freed, 1)

            def route(s):
                with act.Fori(0, HGROUPS) as g:
                    parts_high(s, g)
                act.wait_ge(gate_diff, s + 1)
                s_.activation(top[:, 5, :], top[:, 4, :], ACT.Tanh, scale=0.5 / WSCALE).then_inc(gate_tanh, 1)

            def hidden(s, i, q):
                n = NT * s + i
                act.wait_ge(h1_ready, done(n))
                act.wait_ge(prod_done, freed(n))
                s_.activation(silu[:, q % D_H], bank[:, B_H1 + q % 2, :], ACT.Silu, scale=1.0 / WSCALE)\
                    .then_inc(silu_done, 1)
                act.wait_ge(prod_done, done(n, D_H))
                act.wait_ge(y_ready, freed(n))
                s_.activation(hidh[:, q], prod[:, q % D_H], ACT.Copy).then_inc(hi_done, 1)

            def y_copy(s, q, j):
                i = 4 * j + q
                act.wait_ge(y_ready, done(NT * s + i, D_HID))
                act.wait_ge(y_stored[q], 16 + 16 * io_use(s, q, j))
                s_.activation(yb[:, q].rearrange("p a b -> p (a b)"), bank[:, B_Y + q % 2, 0:2 * D],
                              ACT.Copy).then_inc(y_copied, 1)

            def y_store(s, q, j):
                i = 4 * j + q
                act.wait_ge(y_copied, done(NT * s + i, D_Y))
                act.dma_start(sorted_y[s % 2].rearrange("(t u p) d -> p t u d", p=P, u=2)
                              [:, bass.ds(i, 1)].rearrange("p a u d -> p (a u) d"), yb[:, q])\
                    .then_inc(y_stored[q], 16)

            def experts(s):
                for i in range(LAG):
                    hidden(s, i, i)
                with act.Fori(0, LOOPS) as j:
                    for u in range(4):
                        y_copy(s, u, j)
                        hidden(s, 4 * j + u + LAG, (u + LAG) % 4)
                        y_store(s, u, j)
                for q in range(LAG):
                    y_copy(s, q, LOOPS)
                    y_store(s, q, LOOPS)

            def expert_phase(phase):
                s = 2 * phase
                route(s)
                route(s + 1)
                if phase == 0:
                    for k in range(4):
                        for n, w in enumerate((w1h, w3h, w2h)):
                            act.wait_ge(w_loaded[3 * k + n], 16)
                            s_.activation(w[:, k * 512:(k + 1) * 512], wstage[:, 3 * k + n, :], ACT.Copy,
                                          scale=WSCALE).then_inc(w_hi, 1)
                experts(s)
                experts(s + 1)

            expert_phase(0)

            def q_high(G, par):
                act.wait_ge(m0_ready, done(M0_ATT + 4 * G + 1))
                s_.activation(qksplit[:, par, 1, :], bank[:, B_M0, :], ACT.Copy, scale=1.0 / WSCALE)\
                    .then_inc(m0_hi, 1)

            def k_high(G, par):
                act.wait_ge(m0_ready, done(M0_ATT + 4 * G + 2))
                s_.activation(qksplit[:, par, 2, :], bank[:, B_M0, :], ACT.Copy, scale=1.0 / WSCALE)\
                    .then_inc(m0_hi, 1)

            def v_copy(G, par):
                act.wait_ge(m0_ready, done(M0_ATT + 4 * G + 3))
                s_.activation(vaug[:, par, :, :, 0:DK],
                             bank[:, B_M0, :].rearrange("p (t h d) -> p t h d", t=TILES, d=DK),
                             ACT.Copy, scale=1.0 / WSCALE).then_inc(m0_freed, 1)

            def o_copy(b, q, half):
                act.wait_ge(pv_done, done(4 * b + 2 * half + 1, D_PT))
                s_.activation(ot[:, q % 2, 2 * half:2 * half + 2, :].rearrange("p a b -> p (a b)"),
                             bank[:, B_O, :], ACT.Copy).then_inc(o_copied, 1)

            def o_high(u0):
                act.wait_ge(m1_ready, done(u0 + 2))
                s_.activation(oh[:, :], bank[:, B_M1, 0:SEQ], ACT.Copy).then_inc(oh_done, 1)

            def step(b, q, G, prev=True, scores=True, qkv=True, ln=True):
                for u in range(12):
                    hg, a = divmod(u, 3)
                    v = 4 * b + hg
                    if a == 0:
                        act.wait_ge(pv_done, freed(v))
                    act.wait_ge(st_ready, done(12 * b + u))
                    s_.activation(pt[:, hg, 512 * a:512 * a + 512], bank[:, B_ST + a, :], ACT.Exp,
                                 scale=SM_SCALE).then_inc(exp_done, 1)
                    if u == 3 and prev:
                        o_copy(b - 1, q - 1, 1)
                    if u == 9:
                        if prev:
                            o_high(m1_use(b))
                        o_copy(b, q, 0)
                    if q % 2 == 0 and qkv:
                        par = (q // 2 + 1) % 2
                        if u == 0:
                            q_high(G + 1, par)
                        if u == 2:
                            k_high(G + 1, par)
                        if u == 6:
                            v_copy(G + 1, par)
                    if q % 2 == 1 and ln and u == 10:
                        x_high(m0_use(G + 2), (q // 2) % 2)

            x_high(m0_use(0), 0)
            q_high(0, 0)
            k_high(0, 0)
            act.wait_ge(vaug_set, 2)
            v_copy(0, 0)
            x_high(m0_use(1), 1)
            step(0, 0, 0, prev=False)
            with act.Fori(0, pairs - 1) as i:
                for q in range(1, 5):
                    step(4 * i + q, q, 2 * i + q // 2)
            for q in range(1, 4):
                b = batches - 4 + q
                step(b, q, groups - 2 + q // 2, qkv=q < 2, ln=False)
            o_copy(batches - 1, 3, 1)
            o_high(M1_TAIL)

            expert_phase(1)

        @block.vector
        def _(dve):
            v_ = nc.vector
            dve.sem_inc(prod_done, D_H)
            dve.sem_inc(lo_odd, 1)
            dve.sem_inc(s_reduced, D_S)

            dve.wait_ge(w_hi, 1)
            v_.scalar_tensor_tensor(wsl[:, :], wsmall_f[:, :], WSCALE, wsh[:, :], ALU.mult, ALU.subtract)\
                .then_inc(w_lo, 1)

            def x_tile(t, n=1):
                return X[:, bass.ds(t * D, n * D)]

            def ln_stat(n, t, tile):
                v_.bn_stats(stats[:, t, :], x_tile(tile)).then_inc(ln_stats, 1)

            def ln_mean_of(n, t):
                hold(dve, ln_stats, TILES * n + t + 1)
                v_.bn_aggr(meanvar[:, t, :], stats[:, t, :]).then_inc(ln_mean, 1)

            def normalise(n, t, tile):
                if t == 0:
                    dve.wait_ge(rstd_done, done(n))
                v_.tensor_scalar(xn[:, t, :], x_tile(tile), meanvar[:, t, 0:1], rstd[:, t:t + 1],
                                 ALU.subtract, ALU.mult).then_inc(xn_done, 1)

            def x_low(n_hi, use, par):
                dve.wait_ge(m0_hi, done(n_hi))
                v_.tensor_tensor(xl[:, par, :], bank[:, B_M0, :], xh[:, par, :], ALU.subtract)\
                    .then_inc(m0_freed, 1)

            def hi_use(g):
                return 3 * g

            def layer_norm(g, par):
                n = groups + g
                for t in range(TILES):
                    ln_stat(n, t, TILES * g + t)
                for t in range(TILES):
                    ln_mean_of(n, t)
                for t in range(TILES):
                    normalise(n, t, TILES * g + t)
                x_low(hi_use(g), m0_use(g), par)

            def logits(s, g):
                dve.wait_ge(m0_ready, done(m0_route(s) + 2 * g + 1))
                v_.tensor_copy(logit[:, bass.ds(TILES * g, TILES), :],
                               bank[:, B_M0, 0:TILES * E].rearrange("p (a b) -> p a b", b=E))\
                    .then_inc(m0_freed, 1)

            def parts(s, g, first=False):
                n = HGROUPS * s + g + (groups if s >= 2 else 0)
                tile = HT * (s % 2) + TILES * g
                for t in range(TILES):
                    ln_stat(n, t, tile + t)
                for t in range(TILES):
                    ln_mean_of(n, t)
                for t in range(TILES):
                    if t == 0:
                        dve.wait_ge(rstd_done, done(n))
                    v_.tensor_scalar(xn[:, t, :], x_tile(tile + t), meanvar[:, t, 0:1], rstd[:, t:t + 1],
                                     ALU.subtract, ALU.mult).then_inc(xn_done, 1)
                if not first:
                    logits(s, g - 1)
                dve.wait_ge(xs_hi, HGROUPS * s + g + 1)
                sl = bass.ds(TILES * g, TILES)
                v_.tensor_tensor(xs[:, s % 2, sl, D:2 * D], xn[:, :, :], xs[:, s % 2, sl, 0:D],
                                 ALU.subtract).then_inc(xs_lo, 1)

            def bc(col):
                return col.unsqueeze(2).broadcast_to([P, HT, E])

            def route(s):
                parts(s, 0, first=True)
                if s == 0:
                    dve.wait_ge(x_rest, 16 * (groups - 1))
                with dve.Fori(1, HGROUPS) as g:
                    parts(s, g)
                logits(s, HGROUPS - 1)
                if s == 0:
                    dve.wait_ge(consts, 17)
                count = [0]

                def link(ins):
                    ins.then_inc(gate_step, 1)
                    count[0] += 1
                    dve.wait_ge(gate_step, ROUTE_STEPS * s + count[0])

                def first(src, peak, which, hot):
                    link(v_.tensor_reduce(top[:, peak, :], src[:, :, :], AX.X, ALU.max))
                    link(v_.tensor_tensor(score[:, :, :], src[:, :, :], bc(top[:, peak, :]), ALU.is_equal))
                    link(v_.tensor_tensor(score[:, :, :], score[:, :, :], rank[:, :, :], ALU.mult))
                    link(v_.tensor_reduce(top[:, which, :], score[:, :, :], AX.X, ALU.max))
                    link(v_.tensor_tensor(hot[:, :, :], score[:, :, :], bc(top[:, which, :]), ALU.is_equal))

                dve.wait_ge(m0_freed, m0_route(s) + 2 * HGROUPS)
                first(logit, 0, 1, hot1)
                link(v_.scalar_tensor_tensor(masked[:, :, :], hot1[:, :, :], NEG, logit[:, :, :],
                                             ALU.mult, ALU.add))
                first(masked, 2, 3, hot2)
                v_.tensor_tensor(chosen[:, 0:HT, :], hot1[:, :, :], hot2[:, :, :], ALU.add)\
                    .then_inc(hot_done, 1)
                v_.tensor_tensor(top[:, 4, :], top[:, 0, :], top[:, 2, :], ALU.subtract).then_inc(gate_diff, 1)
                use = m0_route(s) + 2 * HGROUPS
                dve.wait_ge(m0_ready, done(use))
                total = bank[:, B_M0, HT * E:(HT + 1) * E]
                link(v_.tensor_tensor(over[:, :, :], total.unsqueeze(2).broadcast_to([P, E, ETILES]),
                                      bounds[:, :, :], ALU.is_gt))
                link(v_.tensor_reduce(ntiles[:, :], over[:, :, :], AX.X, ALU.add))
                link(v_.tensor_tensor(shares[:, :, :], ntiles[:, :].unsqueeze(1).broadcast_to([P, E, E]),
                                      before[:, :, :], ALU.mult))
                link(v_.tensor_reduce(start[:, :], shares[:, :, :], AX.X, ALU.add))
                link(v_.scalar_tensor_tensor(place[:, :, :],
                                             start[:, :].unsqueeze(1).broadcast_to([P, HT, E]), float(SLOTS),
                                             bank[:, B_M0, 0:HT * E].rearrange("p (a b) -> p a b", b=E),
                                             ALU.mult, ALU.add))
                for k, hot in enumerate((hot1, hot2)):
                    link(v_.tensor_tensor(score[:, :, :], hot[:, :, :], place[:, :, :], ALU.mult))
                    link(v_.tensor_reduce(rowf[:, k, :], score[:, :, :], AX.X, ALU.add))
                v_.tensor_scalar(row[:, s % 2], rowf[:, :, :], 1.0, None, ALU.mult).then_inc(rows_done, 1)
                link(v_.tensor_tensor(passed[:, :, :], tile_no[:, :, :],
                                      start[:, 1:E].unsqueeze(1).broadcast_to([P, NT + 1, E - 1]), ALU.is_ge))
                link(v_.tensor_reduce(expert[:, :], passed[:, :, :], AX.X, ALU.add))
                v_.tensor_scalar(woffset[:, s % 2, :], expert[:, :], float(HID), None, ALU.mult)\
                    .then_inc(tiles_done, 1)
                dve.wait_ge(gate_tanh, s + 1)
                link(v_.tensor_scalar(weight[:, s % 2, 0, :], top[:, 5, :], 1.0, 0.25 / WSCALE,
                                      ALU.add, ALU.mult))
                link(v_.tensor_scalar(weight[:, s % 2, 1, :], top[:, 5, :], -1.0, -0.25 / WSCALE,
                                      ALU.add, ALU.mult))
                dve.sem_inc(gate_step, ROUTE_STEPS - count[0])
                dve.sem_inc(m0_freed, 1)

            def x_copy(s, i, q):
                n = NT * s + i
                dve.wait_ge(t_ready, done(n))
                if not isinstance(i, int):
                    dve.wait_ge(h3_ready, n - 1)
                elif n >= 2:
                    dve.wait_ge(h3_ready, n - min(i, 1))
                v_.tensor_copy(xt[:, q % 2].rearrange("p a b -> p (a b)"), t_bank(q)).then_inc(t_copied, 1)

            def low_part(s, q, j):
                n = NT * s + 4 * j + q
                dve.wait_ge(hi_done, done(n, D_H))
                dve.wait_ge(y_ready, freed(n))
                v_.tensor_tensor(hidl[:, q], prod[:, q % D_H], hidh[:, q], ALU.subtract).then_inc(lo_odd, 1)

            def product(s, q, j):
                i = 4 * j + q
                n = NT * s + i
                dve.wait_ge(h3_ready, done(n))
                dve.wait_ge(silu_done, done(n, D_H))
                dve.wait_ge(hi_done, freed(n))
                dve.wait_ge(lo_odd if q % 2 else lo_even, freed(lo_use(s, q, j)))
                v_.scalar_tensor_tensor(prod[:, q % D_H], bank[:, B_H3 + q % 2, :], 1.0 / WSCALE,
                                        silu[:, q % D_H], ALU.mult, ALU.mult).then_inc(prod_done, 1)

            def add(s, j, u):
                t = units(j, u)
                dve.wait_ge(gathered[u], 32 * (unit_count(s, u) + j + 1))
                tile = HT * (s % 2) + t
                for k in range(2):
                    v_.scalar_tensor_tensor(x_tile(tile), yg[:, u, k, :], weight[:, s % 2, k, bass.ds(t, 1)],
                                            x_tile(tile), ALU.mult, ALU.add).then_inc(x_sum, 1)
                    dve.wait_ge(x_sum, 2 * (HT * s + t) + k + 1)

            def experts(s, side):
                x_copy(s, 0, 0)
                x_copy(s, 1, 1)
                product(s, 0, 0)
                x_copy(s, 2, 2)
                product(s, 1, 0)
                x_copy(s, 3, 3)
                product(s, 2, 0)
                low_part(s, 1, 0)

                def four(j, last=False):
                    for u in range(4):
                        q, jq = (u + LAG) % 4, (j if u == 0 else j + 1)
                        if not (last and u == 3):
                            x_copy(s, 4 * j + u + LAG + 1, u)
                        product(s, q, jq)
                        if side and u < 3:
                            add(s - 1, j, u)
                        if q % 2 == 1:
                            low_part(s, q, jq)

                with dve.Fori(0, LOOPS - 1) as j:
                    four(j)
                four(LOOPS - 1, last=True)
                if side:
                    add(s - 1, LOOPS, 0)

            def expert_phase(phase):
                s = 2 * phase
                route(s)
                route(s + 1)
                if phase == 0:
                    for k in range(4):
                        for n, (hi, lo) in enumerate(((w1h, w1l), (w3h, w3l), (w2h, w2l))):
                            cols = slice(k * 512, (k + 1) * 512)
                            dve.wait_ge(w_hi, 2 + 3 * k + n)
                            v_.scalar_tensor_tensor(lo[:, cols], wstage[:, 3 * k + n, :], WSCALE, hi[:, cols],
                                                    ALU.mult, ALU.subtract).then_inc(w_lo, 1)
                experts(s, False)
                experts(s + 1, True)
                with dve.Fori(0, LOOPS) as j:
                    for u in range(3):
                        add(s + 1, j, u)
                add(s + 1, LOOPS, 0)

            dve.wait_ge(x_first, 16)
            expert_phase(0)
            dve.wait_ge(y_copied, done(2 * NT - 1, D_Y))

            def q_low(G, par):
                dve.wait_ge(m0_hi, done(3 * G + 1))
                v_.scalar_tensor_tensor(qksplit[:, par, 0, :], bank[:, B_M0, :], 1.0 / WSCALE,
                                        qksplit[:, par, 1, :], ALU.mult, ALU.subtract).then_inc(m0_freed, 1)

            def k_low(G, par):
                dve.wait_ge(m0_hi, done(3 * G + 2))
                v_.scalar_tensor_tensor(qksplit[:, par, 3, :], bank[:, B_M0, :], 1.0 / WSCALE,
                                        qksplit[:, par, 2, :], ALU.mult, ALU.subtract).then_inc(m0_freed, 1)

            def row_max(b, q, k):
                hg, kind = divmod(k, 3)
                dve.wait_ge(s_ready, done(12 * b + k))
                src = bank[:, B_S + k % 2, :]
                if kind == 0:
                    dst = negmax[:, q % 2, 0, 4 * hg:4 * hg + 4]
                    src = src.rearrange("p (h k) -> p h k", k=P)
                else:
                    h0 = 4 * hg + 2 * (kind - 1)
                    dst = negmax[:, q % 2, 1, h0:h0 + 2]
                    src = src.rearrange("p (h k) -> p h k", k=SEQ)
                v_.tensor_reduce(dst, src, AX.X, ALU.max, negate=True).then_inc(s_reduced, 1)

            def block_diagonal(G, par):
                dve.wait_ge(zc_done, 192 * (G + 1))
                for j in range(4):
                    v_.tensor_scalar(zk[:, par, :, j, :], zc[:, par, 1, :, :], diag[:, j:j + 1], None,
                                     ALU.mult).then_inc(zk_done, 1)

            def place_max(b, q, use):
                dve.wait_ge(m1_ready, done(use))
                e = q % 2
                v_.tensor_copy(zc[96:100, (q // 2) % 2, 0, :, e * SEQ:(e + 1) * SEQ],
                               bank[96:100, B_M1, :].bitcast(F16).rearrange("p (g q) -> p g q", g=HG))\
                    .then_inc(m1_freed, 1)

            def o_norm(b, u0, qb):
                use = u0 + qb
                view = bank[:, B_M1, :].rearrange("p (h r) -> p h r", r=32)
                dve.wait_ge(m1_ready, done(use))
                v_.reciprocal(rden[:, qb, :], view[:, :, DK]).then_inc(rden_done, 1)
                dve.wait_ge(rden_done, 2 * (b - 1) + qb + 1)
                v_.tensor_tensor(on[:, qb, :].rearrange("p (h d) -> p h d", d=DK), view[:, :, 0:DK],
                                 rden[:, qb, :].unsqueeze(2).broadcast_to([P, HEADS, DK]), ALU.mult)\
                    .then_inc(m1_freed, 1)

            def o_low(b):
                dve.wait_ge(oh_done, b)
                v_.tensor_tensor(ol[:, :], bank[:, B_M1, 0:SEQ], oh[:, :], ALU.subtract).then_inc(m1_freed, 1)

            def x_add(b, u0, tail=False):
                dve.wait_ge(m1_ready, done(u0 + (3 if tail else 4)))
                v_.scalar_tensor_tensor(x_tile(2 * (b - 1), 2), bank[:, B_M1, 0:2 * D], 1.0 / WSCALE,
                                        x_tile(2 * (b - 1), 2), ALU.mult, ALU.add).then_inc(m1_freed, 1)

            def step(b, q, G, prev=True, scores=True, qkv=True, ln=True):
                par = (q // 2 + 1) % 2
                for k in range(12):
                    if scores:
                        row_max(b + 1, q + 1, k)
                    if q % 2 == 0 and qkv and k == 1:
                        q_low(G + 1, par)
                    if q % 2 == 0 and qkv and k == 4:
                        k_low(G + 1, par)
                    if prev and k == 6:
                        o_norm(b, m1_use(b), 0)
                    if prev and k == 9:
                        o_norm(b, m1_use(b), 1)
                    if q % 2 == 1 and ln:
                        n = groups + G + 2
                        tile = TILES * (G + 2)
                        if k in (0, 1, 2, 3):
                            ln_stat(n, k, tile + k)
                        if k in (1, 2, 3, 4):
                            ln_mean_of(n, k - 1)
                        if k in (8, 10):
                            for t in (0, 1) if k == 8 else (2, 3):
                                normalise(n, t, tile + t)
                if prev:
                    o_low(b)
                if scores:
                    place_max(b + 1, q + 1, max_use(b))
                else:
                    no_use(dve, max_use(b), m1_freed)
                if q % 2 == 1 and ln:
                    x_low(hi_use(G + 2), m0_use(G + 2), (q // 2) % 2)
                if prev:
                    x_add(b, m1_use(b))
                else:
                    no_use(dve, max_use(b) + 1, m1_freed)
                if q % 2 == 0 and qkv:
                    block_diagonal(G + 1, par)

            layer_norm(0, 0)
            q_low(0, 0)
            k_low(0, 0)
            layer_norm(1, 1)
            dve.wait_ge(diag_step, 5)
            v_.tensor_reduce(diag[:, :], diag4[:, :, :].rearrange("p r j -> p j r"), AX.X, ALU.max)\
                .then_inc(diag_done, 1)
            dve.wait_ge(diag_done, 1)
            block_diagonal(0, 0)
            for k in range(12):
                row_max(0, 0, k)
            place_max(0, 0, 0)
            step(0, 0, 0, prev=False)
            with dve.Fori(0, pairs - 1) as i:
                for q in range(1, 5):
                    step(4 * i + q, q, 2 * i + q // 2)
            for q in range(1, 4):
                b = batches - 4 + q
                step(b, q, groups - 2 + q // 2, scores=b + 1 < batches, qkv=q < 2, ln=False)
            o_norm(batches, M1_TAIL, 0)
            o_norm(batches, M1_TAIL, 1)
            o_low(batches)
            x_add(batches, M1_TAIL, tail=True)
            dve.wait_ge(m1_freed, M1_TAIL + 4)

            expert_phase(1)

        @block.tensor
        def _(pe):
            t_ = nc.tensor
            pe.sem_inc(y_ready, D_HID)
            pe.sem_inc(pv_done, D_PT)

            def x_transpose(n, use):
                pe.wait_ge(xn_done, TILES * (n + 1))
                if not isinstance(use, int) or use > 0:
                    pe.wait_ge(m0_freed, use)
                for t in range(TILES):
                    last = t_.transpose(bank[:, B_M0, t * P:(t + 1) * P], xn[:, t, :], ident[:, :])
                last.then_inc(m0_ready, 1)

            def split_product(dst, ah, al, bh, bl):
                t_.matmul(dst, ah, bh, start=True, stop=False)
                t_.matmul(dst, ah, bl, start=False, stop=False)
                return t_.matmul(dst, al, bh, start=False, stop=True)

            def group_parts(s, g):
                use = m0_route(s) + 2 * g
                pe.wait_ge(xs_lo, HGROUPS * s + g + 1)
                if not isinstance(use, int) or use > 0:
                    pe.wait_ge(m0_freed, use)
                dst = bank[:, B_M0, :].bitcast(F16)
                for h in range(2):
                    for t in range(TILES):
                        c0 = h * GTOK + t * P
                        last = t_.transpose(dst[:, c0:c0 + P],
                                            xs[:, s % 2, bass.ds(TILES * g + t, 1), h * D:(h + 1) * D]
                                            .rearrange("p a b -> p (a b)"), ident_h[:, :])
                last.then_inc(m0_ready, 1)
                pe.wait_ge(m0_freed, use + 1)
                gate = slice(4 * D, 4 * D + E)
                for t in range(TILES):
                    xh_, xl_ = xth[:, 0, t * P:(t + 1) * P], xth[:, 1, t * P:(t + 1) * P]
                    dst = bank[:, B_M0, t * E:(t + 1) * E]
                    t_.matmul(dst, xh_, wsh[:, gate], start=True, stop=False)
                    t_.matmul(dst, xh_, wsl[:, gate], start=False, stop=False)
                    t_.matmul(dst, xl_, wsh[:, gate], start=False, stop=False)
                    last = t_.matmul(dst, xl_, wsl[:, gate], start=False, stop=True)
                last.then_inc(m0_ready, 1)

            def route(s):
                if s == 0:
                    pe.wait_ge(w_lo, 1)
                group_parts(s, 0)
                with pe.Fori(1, HGROUPS) as g:
                    group_parts(s, g)
                if s == 0:
                    pe.wait_ge(consts, 17)
                pe.wait_ge(hot_done, s + 1)
                pe.wait_ge(m0_freed, m0_route(s) + 2 * HGROUPS)
                dst = bank[:, B_M0, 0:(HT + 1) * E]
                t_.matmul(dst, earlier[:, :], chosen[:, :, :], start=True, stop=False, skip_group_check=True)
                for t in range(HT):
                    last = t_.matmul(dst[:, (t + 1) * E:], ones_b[:, :],
                                     chosen[:, t, :].unsqueeze(1).broadcast_to([P, HT - t, E]),
                                     start=False, stop=t == HT - 1, skip_group_check=True)
                last.then_inc(m0_ready, 1)

            def x_parts(s, i, q, j):
                n = NT * s + i
                pe.wait_ge(xg_loaded[q], 16 * (io_use(s, q, j) + 1))
                if not isinstance(i, int):
                    pe.wait_ge(t_copied, n - 1)
                elif n >= 2:
                    pe.wait_ge(t_copied, n - min(i, 1))
                for h in range(2):
                    for u in range(2):
                        c0 = h * SLOTS + u * P
                        last = t_.transpose(t_bank(q)[:, c0:c0 + P], xg[:, q, u, h * D:(h + 1) * D],
                                            ident_h[:, :])
                last.then_inc(t_ready, 1)

            offset_regs = [pe.alloc_register(f"weight_column{k}") for k in range(2 * D_IO)]

            def weight_columns(s, j, count):
                pe.load(offset_regs[:count], woffset[0:1, s % 2, bass.ds(4 * j, count)])
                return [pe.snap(r, min_val=0, max_val=(E - 1) * HID) for r in offset_regs[:count]]

            def up(s, i, q, off, between=None):
                n = NT * s + i
                pe.wait_ge(t_copied, done(n))
                for ready, read, b0, wh, wl in ((h1_ready, silu_done, B_H1, w1h, w1l),
                                                (h3_ready, prod_done, B_H3, w3h, w3l)):
                    pe.wait_ge(read, freed(n))
                    for c in range(2):
                        cols = bass.ds(off + c * P, P)
                        last = split_product(bank[:, b0 + q % 2, c * SLOTS:(c + 1) * SLOTS],
                                             wh[:, cols], wl[:, cols], xt[:, q % 2, 0], xt[:, q % 2, 1])
                    last.then_inc(ready, 1)
                    if between is not None and ready is h1_ready:
                        x_parts(*between)

            def down(s, q, j, off):
                i = 4 * j + q
                n = NT * s + i
                pe.wait_ge(hi_done, done(n, D_H))
                pe.wait_ge(y_copied, freed(n))
                pe.wait_ge(lo_odd if q % 2 else lo_even, done(lo_use(s, q, j), 1))
                for u in range(2):
                    dst = bank[:, B_Y + q % 2, u * D:(u + 1) * D]
                    for c in range(2):
                        toks = slice(c * SLOTS + u * P, c * SLOTS + (u + 1) * P)
                        cols = bass.ds(off + c * D, D)
                        hh, hl = hidh[:, q, toks], hidl[:, q, toks]
                        t_.matmul(dst, hh, w2h[:, cols], start=c == 0, stop=False)
                        t_.matmul(dst, hh, w2l[:, cols], start=False, stop=False)
                        last = t_.matmul(dst, hl, w2h[:, cols], start=False, stop=c == 1)
                last.then_inc(y_ready, 1)

            def experts(s):
                pe.wait_ge(tiles_done, s + 1)
                if s > 0:
                    pe.wait_ge(y_copied, done(NT * s - 1, D_Y))
                x_parts(s, 0, 0, 0)
                x_parts(s, 1, 1, 0)
                off = weight_columns(s, 0, 4)
                up(s, 0, 0, off[0], between=(s, 2, 2, 0))
                up(s, 1, 1, off[1], between=(s, 3, 3, 0))
                up(s, 2, 2, off[2])

                def four(j, last=False):
                    off = weight_columns(s, j, 8)
                    for u in range(4):
                        down(s, u, j, off[u])
                        i = 4 * j + u + LAG
                        up(s, i, (u + LAG) % 4, off[u + LAG],
                           between=None if last and u == 3 else (s, i + 1, u, j + 1))

                with pe.Fori(0, LOOPS - 1) as j:
                    four(j)
                four(LOOPS - 1, last=True)
                off = weight_columns(s, LOOPS, 4)
                for q in range(LAG):
                    down(s, q, LOOPS, off[q])

            def expert_phase(phase):
                s = 2 * phase
                route(s)
                route(s + 1)
                if phase == 0:
                    pe.wait_ge(w_lo, 13)
                pe.wait_ge(m0_freed, m0_route(s + 1) + ROUTE_USES)
                experts(s)
                experts(s + 1)

            pe.wait_ge(consts, 6)
            expert_phase(0)

            pe.wait_ge(y_copied, done(2 * NT - 1, D_Y))
            WQ, WK, WV, WO = (slice(k * D, (k + 1) * D) for k in range(4))

            def project(G, par, which):
                use = m0_use(G) + 1 + which
                pe.wait_ge(m0_freed, use)
                if which < 2:
                    w = (WQ, WK)[which]
                    last = split_product(bank[:, B_M0, :], wsh[:, w], wsl[:, w], xh[:, par, :], xl[:, par, :])
                else:
                    for t in range(TILES):
                        toks = slice(t * P, (t + 1) * P)
                        last = split_product(bank[:, B_M0, toks], xh[:, par, toks], xl[:, par, toks],
                                             wsh[:, WV], wsl[:, WV])
                last.then_inc(m0_ready, 1)

            def scores(b, q, k, G_z=None):
                hg, kind = divmod(k, 3)
                par, e = (q // 2) % 2, q % 2
                if G_z is not None:
                    pe.wait_ge(zc_done, 192 * (G_z + 1))
                    pe.wait_ge(zk_done, 4 * (G_z + 1))
                pe.wait_ge(s_reduced, freed(12 * b + k))
                dst = bank[:, B_S + k % 2, :]
                q0 = e * SEQ + (0 if kind == 0 else P)
                qs = zc[0:96, par, 0, hg, q0:q0 + P]
                if kind == 0:
                    t_.matmul(dst, qs, zk[0:96, par, hg, :, e * SEQ:e * SEQ + P], start=True, stop=False)
                    t_.matmul(dst, ident_b[:, :], causal[:, :, :], start=False, stop=True)\
                        .then_inc(s_ready, 1)
                else:
                    j = 2 * (kind - 1)
                    t_.matmul(dst, qs, zk[0:96, par, hg, j:j + 2, e * SEQ:(e + 1) * SEQ],
                              start=True, stop=False, skip_group_check=True)
                    t_.matmul(dst.rearrange("p (h k) -> p h k", k=SEQ)[:, :, P:SEQ], ident_b[:, :],
                              causal[:, 0:2, :], start=False, stop=True, skip_group_check=True)\
                        .then_inc(s_ready, 1)

            def max_transpose(b, q, use):
                pe.wait_ge(clamp_done, done(b))
                if not isinstance(use, int) or use > 0:
                    pe.wait_ge(m1_freed, use)
                dst = bank[96:100, B_M1, :].bitcast(F16)
                for qb in range(2):
                    for hg in range(HG):
                        last = t_.transpose(dst[:, hg * SEQ + qb * P:hg * SEQ + qb * P + P],
                                            negmax_h[:, q % 2, qb, 4 * hg:4 * hg + 4], ident_h[:, :])
                last.then_inc(m1_ready, 1)

            def scores_t(b, q, u):
                hg, a = divmod(u, 3)
                par, e = (q // 2) % 2, q % 2
                if u == 0:
                    pe.wait_ge(m1_freed, done(0 if isinstance(b, int) and b == 0 else max_use(b - 1)))
                pe.wait_ge(exp_done, freed(12 * b + u))
                dst = bank[:, B_ST + a, :]
                k0 = e * SEQ + (0 if a < 2 else P)
                heads = (0, 1) if a == 0 else (2, 3) if a == 1 else (0, 1, 2, 3)
                nq = SEQ if a < 2 else P
                for m, j in enumerate(heads):
                    last = t_.matmul(dst[:, m * nq:(m + 1) * nq], zk[:, par, hg, j, k0:k0 + P],
                                     zc[:, par, 0, hg, (e + 1) * SEQ - nq:(e + 1) * SEQ],
                                     start=True, stop=True)
                last.then_inc(st_ready, 1)

            def values(b, q, hg):
                v = 4 * b + hg
                par, e = (q // 2) % 2, q % 2
                pe.wait_ge(sel_done, 2 * v + 2)
                if hg % 2 == 0:
                    pe.wait_ge(o_copied, freed(2 * b + hg // 2))
                c0 = (hg % 2) * SEQ
                buf = pt[:, hg]
                for j in range(4):
                    t_.matmul(bank[32 * j:32 * j + 32, B_O, c0:c0 + SEQ], vaug[:, par, 2 * e, 4 * hg + j, :],
                              buf[:, j * SEQ:(j + 1) * SEQ], start=True, stop=False, skip_group_check=True)
                for j in range(4):
                    last = t_.matmul(bank[32 * j:32 * j + 32, B_O, c0 + P:c0 + SEQ],
                                     vaug[:, par, 2 * e + 1, 4 * hg + j, :],
                                     buf[:, 1024 + j * P:1024 + (j + 1) * P], start=False, stop=True,
                                     skip_group_check=True)
                last.then_inc(pv_done, 1)

            def o_back(b, q, u0, qb):
                use = u0 + qb
                pe.wait_ge(o_copied, done(2 * (b - 1) + 1, D_O))
                pe.wait_ge(m1_freed, use)
                for hg in range(HG):
                    last = t_.transpose(bank[:, B_M1, hg * P:(hg + 1) * P],
                                        ot[:, (q - 1) % 2, hg, qb * P:(qb + 1) * P], ident[:, :])
                last.then_inc(m1_ready, 1)

            def o_transpose(u0):
                use = u0 + 2
                pe.wait_ge(m1_freed, use)
                for qb in range(2):
                    last = t_.transpose(bank[:, B_M1, qb * P:(qb + 1) * P], on[:, qb, :], ident[:, :])
                last.then_inc(m1_ready, 1)

            def o_project(u0, tail=False):
                use = u0 + 3 + (0 if tail else 1)
                pe.wait_ge(m1_freed, use)
                for qb in range(2):
                    toks = slice(qb * P, (qb + 1) * P)
                    last = split_product(bank[:, B_M1, toks], oh[:, toks], ol[:, toks], wsh[:, WO], wsl[:, WO])
                last.then_inc(m1_ready, 1)

            def step(b, q, G, prev=True, more=True, qkv=True, ln=True):
                issued = 0
                for u in range(12):
                    quota = min(12, -(-(u + 1) * 12 // 9))
                    while more and issued < quota:
                        scores(b + 1, q + 1, issued, (G + 1 if q % 2 == 1 else None) if issued == 0 else None)
                        issued += 1
                    scores_t(b, q, u)
                    fresh = q % 2 == 0 and qkv
                    if fresh and u == 0:
                        project(G + 1, (q // 2 + 1) % 2, 0)
                    if fresh and u == 2:
                        project(G + 1, (q // 2 + 1) % 2, 1)
                    if u == 2 and prev:
                        values(b - 1, q - 1, 3)
                    if u == 3 and prev:
                        o_back(b, q, m1_use(b), 0)
                    if u == 5:
                        values(b, q, 0)
                        if prev:
                            o_back(b, q, m1_use(b), 1)
                        if fresh:
                            project(G + 1, (q // 2 + 1) % 2, 2)
                    if u == 7 and prev:
                        o_transpose(m1_use(b))
                    if u == 8:
                        values(b, q, 1)
                    if u == 9 and q % 2 == 1 and ln:
                        x_transpose(groups + G + 2, m0_use(G + 2))
                    if u == 10:
                        if more:
                            max_transpose(b + 1, q + 1, max_use(b))
                        else:
                            pe.wait_ge(m1_freed, max_use(b))
                            no_use(pe, max_use(b), m1_ready)
                    if u == 11:
                        values(b, q, 2)
                        if prev:
                            o_project(m1_use(b))
                        else:
                            pe.wait_ge(m1_freed, max_use(b) + 1)
                            no_use(pe, max_use(b) + 1, m1_ready)

            x_transpose(groups, m0_use(0))
            for which in range(3):
                project(0, 0, which)
            x_transpose(groups + 1, m0_use(1))
            pe.wait_ge(vaug_set, 2)
            for k in range(12):
                scores(0, 0, k, 0 if k == 0 else None)
            max_transpose(0, 0, 0)
            step(0, 0, 0, prev=False)
            with pe.Fori(0, pairs - 1) as i:
                for q in range(1, 5):
                    step(4 * i + q, q, 2 * i + q // 2)
            for q in range(1, 4):
                b = batches - 4 + q
                step(b, q, groups - 2 + q // 2, more=b + 1 < batches, qkv=q < 2, ln=False)
            values(batches - 1, 3, 3)
            o_back(batches, 0, M1_TAIL, 0)
            o_back(batches, 0, M1_TAIL, 1)
            o_transpose(M1_TAIL)
            o_project(M1_TAIL, tail=True)

            pe.wait_ge(exp_done, done(12 * batches - 1, D_ST))
            pe.wait_ge(m1_freed, M1_TAIL + 4)
            expert_phase(1)


_INS = ("x_in", "w_up1", "w_up3", "w_down", "w_small")


def kernel(L0_attn_x, L0_attn_WQ, L0_attn_WK, L0_attn_WV, L0_attn_WO, L0_ffn_gate_w, L0_ffn_w1,
           L0_ffn_w2, L0_ffn_w3):
    import concourse.bacc as bacc
    from concourse.bass_utils import run_bass_kernel_spmd

    x = np.asarray(L0_attn_x)
    batches, seq, d = x.shape
    assert (seq, d) == (SEQ, D)
    w1 = np.asarray(L0_ffn_w1).reshape(E * HID, D).T
    w3 = np.asarray(L0_ffn_w3).reshape(E * HID, D).T
    w2 = np.asarray(L0_ffn_w2).transpose(0, 2, 1).reshape(CHUNKS, P, D).transpose(1, 0, 2).reshape(P, -1)
    small = np.concatenate([np.asarray(w) for w in (L0_attn_WQ, L0_attn_WK, L0_attn_WV, L0_attn_WO)]
                           + [np.asarray(L0_ffn_gate_w).T], axis=1)
    arrays = dict(zip(_INS, (np.ascontiguousarray(a) for a in (x.reshape(-1, D), w1, w3, w2, small))))

    nc = bacc.Bacc("TRN2", target_bir_lowering=False, num_devices=1)
    args = [nc.dram_tensor(n, arrays[n].shape, F32, kind="ExternalInput").ap() for n in _INS]
    out = nc.dram_tensor("out", (batches * SEQ, D), F32, kind="ExternalOutput").ap()
    build_macaron(nc, *args, out, batches)
    r = run_bass_kernel_spmd(nc, [arrays], core_ids=[0])
    return r.results[0]["out"].reshape(batches, SEQ, D)
```

```python
from contextlib import ExitStack

import numpy as np

import concourse.bass as bass
from concourse import mybir

F32 = mybir.dt.float32
F16 = mybir.dt.float16
BF16 = mybir.dt.bfloat16
I32 = mybir.dt.int32
ALU = mybir.AluOpType
ACT = mybir.ActivationFunctionType
AX = mybir.AxisListType

P = 128
D = 128
SEQ = 256
HEADS, DK = 16, 8
E, HID = 8, 256
TILES = 4
GTOK = TILES * P
CHUNKS = E * HID // P
LAG = 3
HG = 4
WSCALE = 256.0
EPS = 1e-5
NEG = -1.0e30
MLIMIT = 60000.0
SM_SCALE = DK ** -0.5

SLOTS = 256
HT = 16
HGROUPS = HT // TILES
HTOK = HT * P
NT = (2 * HTOK + E * (SLOTS - 1)) // SLOTS
ETILES = HTOK // SLOTS
LOOPS = (NT - LAG) // 4
assert NT == 4 * LOOPS + LAG
ROUTE_STEPS = 23
ROUTE_USES = 2 * HGROUPS + 1

D_H = 2
D_HID = 4
D_Y = 1
D_IO = 4
D_YG = 4
D_S = 2
D_ST = 3
D_PT = 4
D_O = 1


def freed(n):
    return n + 1


def done(n, depth=0):
    return n + 1 + depth


def build_macaron(nc, x_in, w_up1, w_up3, w_down, w_small, out, batches):
    groups = batches * SEQ // GTOK
    assert batches == 2 * groups and groups == 2 * HGROUPS
    rows = NT * SLOTS
    sorted_x = [nc.dram_tensor(f"sorted_x{k}", (rows, 2 * D), F16, kind="Internal").ap() for k in range(2)]
    sorted_y = [nc.dram_tensor(f"sorted_y{k}", (rows, D), F32, kind="Internal").ap() for k in range(2)]
    ctx = ExitStack()
    with ctx:
        def sb(name, shape, dt):
            return ctx.enter_context(nc.sbuf_tensor(name, shape, dt))

        def sem(name):
            return ctx.enter_context(nc.semaphore(name))

        X = sb("X", [P, groups * TILES * D], F32)
        w1h = sb("w1h", [P, E * HID], F16)
        w1l = sb("w1l", [P, E * HID], F16)
        w3h = sb("w3h", [P, E * HID], F16)
        w3l = sb("w3l", [P, E * HID], F16)
        w2h = sb("w2h", [P, CHUNKS * D], F16)
        w2l = sb("w2l", [P, CHUNKS * D], F16)
        NSMALL = 4 * D + E
        wsh = sb("wsh", [P, NSMALL], F16)
        wsl = sb("wsl", [P, NSMALL], F16)
        wsmall_f = sb("wsmall_f", [P, NSMALL], F32)
        ident = sb("ident", [P, P], F32)
        ident_h = sb("ident_h", [P, P], F16)
        ident_b = sb("ident_b", [P, P], BF16)
        causal = sb("causal", [P, 4, P], BF16)
        causal_t = sb("causal_t", [P, 4, P], BF16)
        rank = sb("rank", [P, HT, E], F32)
        earlier = sb("earlier", [P, P], BF16)
        ones_b = sb("ones_b", [P, P], BF16)
        zeros = sb("zeros", [P, 2 * D], F16)
        bounds = sb("bounds", [P, E, ETILES], F32)
        before = sb("before", [P, E, E], F32)
        tile_no = sb("tile_no", [P, NT + 1, E - 1], F32)
        stats = sb("stats", [P, TILES, 6], F32)
        meanvar = sb("meanvar", [P, TILES, 2], F32)
        var_eps = sb("var_eps", [P, TILES], F32)
        minus_half = sb("minus_half", [P, TILES], F32)
        rstd = sb("rstd", [P, TILES], F32)
        xn = sb("xn", [P, TILES, D], F32)
        xh = sb("xh", [P, 2, GTOK], F16)
        xl = sb("xl", [P, 2, GTOK], F16)
        r_stats = sb("r_stats", [P, HGROUPS, TILES, 6], F32)
        r_meanvar = sb("r_meanvar", [P, HGROUPS, TILES, 2], F32)
        r_var_eps = sb("r_var_eps", [P, TILES], F32)
        r_rstd = sb("r_rstd", [P, HGROUPS, TILES], F32)
        r_xn = sb("r_xn", [P, TILES, D], F32)
        row_now = sb("row_now", [P, D_YG, 2], I32)
        xs = sb("xs", [P, 2, HT, 2 * D], F16)
        xth = sb("xth", [P, 2, GTOK], F16)
        logit = sb("logit", [P, HT, E], F32)
        masked = sb("masked", [P, HT, E], F32)
        score = sb("score", [P, HT, E], F32)
        hot1 = sb("hot1", [P, HT, E], F32)
        hot2 = sb("hot2", [P, HT, E], F32)
        top = sb("top", [P, 6, HT], F32)
        chosen = sb("chosen", [P, HT + 1, E], BF16)
        over = sb("over", [P, E, ETILES], F32)
        ntiles = sb("ntiles", [P, E], F32)
        shares = sb("shares", [P, E, E], F32)
        start = sb("start", [P, E], F32)
        passed = sb("passed", [P, NT + 1, E - 1], F32)
        expert = sb("expert", [P, NT + 1], F32)
        woffset = sb("woffset", [P, 2, NT + 1], I32)
        place = sb("place", [P, HT, E], F32)
        rowf = sb("rowf", [P, 2, HT], F32)
        row = sb("row", [P, 2, 2, HT], I32)
        weight = sb("weight", [P, 2, 2, HT], F32)
        yg = sb("yg", [P, D_YG, 2, D], F32)
        qksplit = sb("qksplit", [P, 2, 4, GTOK], F16)
        zc = sb("zc", [P, 2, 2, HG, GTOK], F16)
        zk = sb("zk", [P, 2, HG, 4, GTOK], F16)
        diag4 = sb("diag4", [P, 4, 4], F32)
        diag = sb("diag", [P, 4], F32)
        vaug = sb("vaug", [P, 2, TILES, HEADS, 32], F32)
        negmax = sb("negmax", [P, 2, 2, HEADS], F32)
        negmax_h = sb("negmax_h", [P, 2, 2, HEADS], F16)
        pt_flat = sb("pt", [P, D_PT * 3 * 512], F32)
        pt = pt_flat[:, :].rearrange("p (a b) -> p a b", a=D_PT)
        ot = sb("ot", [P, 2, HG, SEQ], F32)
        rden = sb("rden", [P, 2, HEADS], F32)
        on = sb("on", [P, 2, D], F32)
        oh = sb("oh", [P, SEQ], F16)
        ol = sb("ol", [P, SEQ], F16)
        wstage = pt_flat[:, :].rearrange("p (k n) -> p k n", n=512)
        taken = [0]

        def part_of(n, shape, dt=F16):
            size = n * int(np.prod(shape)) // (1 if dt is F32 else 2)
            cols = pt_flat[:, taken[0]:taken[0] + size]
            taken[0] += size
            assert taken[0] <= D_PT * 3 * 512
            if dt is not F32:
                cols = cols.bitcast(dt)
            if len(shape) == 1:
                return cols.rearrange("p (n a) -> p n a", n=n)
            return cols.rearrange("p (n a b) -> p n a b", n=n, a=shape[0])

        silu = part_of(D_H, [2 * SLOTS], F32)
        prod = part_of(D_H, [2 * SLOTS], F32)
        hidh = part_of(D_HID, [2 * SLOTS])
        hidl = part_of(D_HID, [2 * SLOTS])
        xt = part_of(2, [2, SLOTS])
        xg = part_of(D_IO, [2, 2 * D])
        yb = zk[:, 1, 0, 0:4, :].rearrange("p j n -> p (j n)").bitcast(F32)\
            .rearrange("p (q u d) -> p q u d", q=D_IO, u=2)

        bank = ctx.enter_context(nc.psum_tensor("bank", [P, 8, 512], F32))
        B_H1, B_H3, B_Y = 0, 2, 4
        B_T = 5, 7
        B_S, B_ST, B_O = 0, 2, 5
        B_M0, B_M1 = 6, 7

        def t_bank(q):
            return bank[:, B_T[q % 2], 0:SLOTS].bitcast(F16)

        x_first = sem("x_first")
        x_rest = sem("x_rest")
        small_loaded = sem("small_loaded")
        w_loaded = [sem(f"w_loaded{k}") for k in range(12)]
        w_hi = sem("w_hi")
        w_lo = sem("w_lo")
        consts = sem("consts")
        ln_stats = sem("ln_stats")
        ln_mean = sem("ln_mean")
        eps_added = sem("eps_added")
        rstd_done = sem("rstd_done")
        xn_done = sem("xn_done")
        m0_ready = sem("m0_ready")
        m0_hi = sem("m0_hi")
        m0_freed = sem("m0_freed")
        h1_ready = sem("h1_ready")
        h3_ready = sem("h3_ready")
        silu_done = sem("silu_done")
        prod_done = sem("prod_done")
        hi_done = sem("hi_done")
        lo_done = sem("lo_done")
        y_ready = sem("y_ready")
        y_copied = sem("y_copied")
        t_ready = sem("t_ready")
        t_copied = sem("t_copied")
        r_stated = sem("r_stated")
        r_mean = sem("r_mean")
        r_eps_added = sem("r_eps_added")
        r_rstd_done = sem("r_rstd_done")
        r_xn_done = sem("r_xn_done")
        row_copied = sem("row_copied")
        xs_hi = sem("xs_hi")
        xs_lo = sem("xs_lo")
        gate_step = sem("gate_step")
        gate_diff = sem("gate_diff")
        gate_tanh = sem("gate_tanh")
        hot_done = sem("hot_done")
        rows_done = sem("rows_done")
        tiles_done = sem("tiles_done")
        zeroed = sem("zeroed")
        scattered = [sem("scattered0"), sem("scattered1")]
        xg_loaded = [sem(f"xg_loaded{k}") for k in range(D_IO)]
        y_stored = [sem(f"y_stored{k}") for k in range(D_IO)]
        gathered = [sem(f"gathered{k}") for k in range(D_YG)]
        x_sum = sem("x_sum")
        s_ready = sem("s_ready")
        s_reduced = sem("s_reduced")
        clamp_done = sem("clamp_done")
        st_ready = sem("st_ready")
        exp_done = sem("exp_done")
        pv_done = sem("pv_done")
        o_copied = sem("o_copied")
        m1_ready = sem("m1_ready")
        m1_freed = sem("m1_freed")
        oh_done = sem("oh_done")
        rden_done = sem("rden_done")
        zc_done = [sem("zc_done0"), sem("zc_done1")]
        zk_done = sem("zk_done")
        vaug_set = sem("vaug_set")
        diag_step = sem("diag_step")
        diag_done = sem("diag_done")
        out_done = sem("out_done")
        held = sem("held")

        def hold(eng, what, value):
            eng.wait_ge(what, value)
            eng.sem_inc(held, 1)

        def no_use(eng, use, count):
            if count is m1_freed:
                eng.wait_ge(m1_freed, use)
                eng.wait_ge(m1_ready, use + 1)
            eng.sem_inc(count, 1)

        def unit_count(s, k):
            return s * (HT // D_YG)

        CONSTS = 23
        block = ctx.enter_context(nc.Block())

        M0_ATT = 2 * ROUTE_USES

        FIRST = batches - 2 * HGROUPS + 1
        ROUTED = FIRST + HGROUPS
        assert FIRST == 2 * HGROUPS + 1 and FIRST % 2 == 1

        late = {}
        n_use = M0_ATT + 4 * (FIRST // 2 + 2) + 1
        for b in range(FIRST, batches + 1):
            G = b // 2
            if b % 2 == 1 and G + 2 < groups:
                late["qkv", G + 2, 1], late["qkv", G + 2, 2] = n_use, n_use + 1
                n_use += 2
            if b % 2 == 0 and G + 1 < groups:
                late["qkv", G + 1, 3] = n_use
                n_use += 1
            if b == ROUTED:
                late["sums", 2] = n_use
                n_use += 1
            late["route", b - FIRST] = n_use
            n_use += 2
            if b % 2 == 0 and G + 2 < groups:
                late["qkv", G + 2, 0] = n_use
                n_use += 1
        late["sums", 3] = n_use

        def m0_route(s, g):
            return ROUTE_USES * s + 2 * g if s < 2 else late["route", HGROUPS * (s - 2) + g]

        def m0_sums(s):
            return ROUTE_USES * (s + 1) - 1 if s < 2 else late["sums", s]

        def m0_use(g, which=0):
            if isinstance(g, int) and ("qkv", g, which) in late:
                return late["qkv", g, which]
            return M0_ATT + 4 * g + which

        def rounds(eng, s, four):
            for j in range(EARLY_ROUNDS[s]):
                four(j)
            with eng.Fori(EARLY_ROUNDS[s], LOOPS - 1) as j:
                four(j)
            four(LOOPS - 1, last=True)

        def io_use(s, q, j):
            return s * (LOOPS + (1 if q < LAG else 0)) + j

        def add_units(i, q):
            return [(8 * i + v, v % D_YG, 2 * i + v // D_YG) for v in (2 * q - 2, 2 * q - 1)]

        def b_ok(b):
            return not isinstance(b, int) or b < batches

        def G_ok(g):
            return not isinstance(g, int) or g < groups

        AHEAD = 4

        def score_bank(b, q, u):
            k = AHEAD + u
            seq, pos = (b + 1, q + 1) if k < 12 else (b + 2, q + 2)
            return None if isinstance(seq, int) and seq >= batches else (seq, pos, k % 12)

        def route_of(b):
            return 2 + (b - FIRST) // HGROUPS, (b - FIRST) % HGROUPS

        EARLY_ROUNDS = (0, 0, 2, 0)

        def m1_use(b):
            return 5 * b - 2

        def max_use(b):
            return m1_use(b) + 3

        M1_TAIL = m1_use(batches)

        @block.sync
        def _(sp):
            xv = x_in.rearrange("(t p) d -> p t d", p=P)
            Xv = X[:, :].rearrange("p (t d) -> p t d", d=D)
            sp.dma_start(Xv[:, 0:TILES, :], xv[:, 0:TILES, :]).then_inc(x_first, 16)
            sp.dma_start(wsmall_f[:, :], w_small).then_inc(small_loaded, 16)
            for g in range(1, groups):
                sp.dma_start(Xv[:, g * TILES:(g + 1) * TILES, :], xv[:, g * TILES:(g + 1) * TILES, :])\
                    .then_inc(x_rest, 16)
            sp.wait_ge(consts, 1)
            for k in range(2):
                sp.dma_start(sorted_x[k].rearrange("(t p) d -> p t d", p=P),
                             zeros[:, :].unsqueeze(1).broadcast_to([P, rows // P, 2 * D])).then_inc(zeroed, 16)
                if k == 0:
                    for m in range(4):
                        for n, w in enumerate((w_up1, w_up3, w_down)):
                            sp.dma_start(wstage[:, 3 * m + n, :], w[:, m * 512:(m + 1) * 512])\
                                .then_inc(w_loaded[3 * m + n], 16)

            def load(s, q, j):
                i = 4 * j + q
                if not isinstance(j, int) or j > 0:
                    hold(sp, t_ready, NT * s + i - D_IO + 1)
                sp.dma_start(xg[:, q], sorted_x[s % 2].rearrange("(t u p) d -> p t u d", p=P, u=2)
                             [:, bass.ds(i, 1)].rearrange("p a u d -> p (a u) d")).then_inc(xg_loaded[q], 16)

            def store(s, q, j):
                i = 4 * j + q
                hold(sp, y_copied, done(NT * s + i, D_Y))
                sp.dma_start(sorted_y[s % 2].rearrange("(t u p) d -> p t u d", p=P, u=2)
                             [:, bass.ds(i, 1)].rearrange("p a u d -> p (a u) d"), yb[:, q])\
                    .then_inc(y_stored[q], 16)

            def first_load(s, q):
                if s > 0:
                    sp.wait_ge(t_ready, NT * (s - 1) + (4 * LOOPS if q < LAG else 4 * LOOPS - 4) + q + 1)
                if q == 0:
                    sp.wait_ge(scattered[s % 2], 16 * 2 * HT * (s // 2 + 1))
                    if s >= 2:
                        for k in range(D_YG):
                            sp.wait_ge(gathered[k], 32 * unit_count(s - 1, k))
                load(s, q, 0)

            def experts(s):
                for q in range(D_IO):
                    load(s, q, 1)
                with sp.Fori(2, LOOPS) as j:
                    for q in range(D_IO):
                        load(s, q, j)
                        store(s, q, j - 2)
                for q in range(D_IO):
                    if q < LAG:
                        load(s, q, LOOPS)
                    store(s, q, LOOPS - 2)
                for q in range(D_IO):
                    store(s, q, LOOPS - 1)
                    if s % 2 == 0:
                        first_load(s + 1, q)
                for q in range(LAG):
                    store(s, q, LOOPS)

            sp.wait_ge(w_lo, 13)
            for q in range(D_IO):
                first_load(0, q)
            experts(0)
            experts(1)

            sp.wait_ge(consts, CONSTS)

            def stack(g, par):
                hold(sp, m0_freed, m0_use(g, 2) + 1)
                if not isinstance(g, int) or g > 1:
                    hold(sp, st_ready, 24 * (g - 1))
                for half in range(2):
                    if not isinstance(g, int) or g > 0:
                        hold(sp, zc_done[half], 96 * g)
                for hg in range(HG):
                    rows = qksplit[32 * hg:32 * hg + 32, par]
                    for r, parts in enumerate((rows[:, 1:3], rows[:, 1:4:2], rows[:, 0:3:2])):
                        sp.dma_start(zc[32 * r:32 * r + 32, par, :, hg, :], parts).then_inc(zc_done[hg // 2], 16)

            stack(0, 0)
            stack(1, 1)
            with sp.Fori(0, FIRST // 4) as i:
                stack(2 * i + 2, 0)
                stack(2 * i + 3, 1)
            stack(groups - 2, 0)
            stack(groups - 1, 1)

            sp.wait_ge(pv_done, done(4 * batches - 1, D_PT))
            for q in range(D_IO):
                first_load(2, q)
            experts(2)
            experts(3)
            ov = out.rearrange("(t p) d -> p t d", p=P)
            with sp.Fori(0, groups) as g:
                hold(sp, x_sum, 2 * 2 * groups * TILES - 2 * TILES * (groups - 1) + 2 * TILES * g)
                sp.dma_start(ov[:, bass.ds(TILES * g, TILES), :], Xv[:, bass.ds(TILES * g, TILES), :])\
                    .then_inc(out_done, 16)
            sp.wait_ge(out_done, 16 * groups)

        @block.gpsimd
        def _(pool):
            ps = nc.gpsimd
            ps.memset(zeros[:, :], 0.0).then_inc(consts, 1)
            ps.memset(minus_half[:, :], -0.5).then_inc(consts, 1)
            ps.memset(ident[:, :], 0.0).then_inc(consts, 1)
            pool.wait_ge(consts, 3)
            ps.affine_select(out=ident[:, :], in_=ident[:, :], compare_op=ALU.not_equal, fill=1.0, base=0,
                             pattern=[[-1, P]], channel_multiplier=1).then_inc(consts, 1)
            pool.wait_ge(consts, 4)
            ps.tensor_copy(ident_h[:, :], ident[:, :]).then_inc(consts, 1)
            ps.tensor_copy(ident_b[:, :], ident[:, :]).then_inc(consts, 1)

            def routing_constants():
                ps.iota(rank[:, :, :], pattern=[[0, HT], [-1, E]], base=E, channel_multiplier=0,
                        allow_small_or_imprecise_dtypes=True).then_inc(consts, 1)
                ps.memset(ones_b[:, :], 1.0).then_inc(consts, 1)
                ps.memset(earlier[:, :], 1.0).then_inc(consts, 1)
                ps.memset(chosen[:, HT, :], 0.0).then_inc(consts, 1)
                ps.memset(before[:, :, :], 1.0).then_inc(consts, 1)
                ps.iota(bounds[:, :, :], pattern=[[0, E], [SLOTS, ETILES]], base=0, channel_multiplier=0,
                        allow_small_or_imprecise_dtypes=True).then_inc(consts, 1)
                ps.iota(tile_no[:, :, :], pattern=[[1, NT + 1], [0, E - 1]], base=0, channel_multiplier=0,
                        allow_small_or_imprecise_dtypes=True).then_inc(consts, 1)
                ps.memset(causal[:, :, :], 0.0).then_inc(consts, 1)
                ps.memset(causal_t[:, :, :], 0.0).then_inc(consts, 1)
                pool.wait_ge(consts, 15)
                ps.affine_select(out=earlier[:, :], in_=earlier[:, :], compare_op=ALU.is_ge, fill=0.0,
                                 base=-1, pattern=[[1, P]], channel_multiplier=-1).then_inc(consts, 1)
                ps.affine_select(out=before[:, :, :], in_=before[:, :, :], compare_op=ALU.is_ge, fill=0.0,
                                 base=-1, pattern=[[1, E], [-1, E]], channel_multiplier=0).then_inc(consts, 1)
                ps.affine_select(out=causal[:, :, :], in_=causal[:, :, :], compare_op=ALU.is_ge, fill=NEG,
                                 base=0, pattern=[[0, 4], [-1, P]], channel_multiplier=1).then_inc(consts, 1)
                ps.affine_select(out=causal_t[:, :, :], in_=causal_t[:, :, :], compare_op=ALU.is_ge, fill=NEG,
                                 base=0, pattern=[[0, 4], [1, P]], channel_multiplier=-1).then_inc(consts, 1)

            def attention_constants():
                for par in range(2):
                    ps.memset(zc[:, par, 0].rearrange("p a b -> p (a b)").bitcast(F32), 0.0)\
                        .then_inc(consts, 1)
                    ps.memset(zc[:, par, 1], 1.0).then_inc(consts, 1)
                ps.memset(vaug[:, :], 0.0).then_inc(vaug_set, 1)
                pool.wait_ge(vaug_set, 1)
                ps.memset(vaug[:, :, :, :, DK:DK + 1], 1.0).then_inc(vaug_set, 1)
                ps.memset(diag4[:, :, :], 1.0).then_inc(diag_step, 1)
                pool.wait_ge(diag_step, 1)
                ps.memset(diag4[:, 3, :], 0.0).then_inc(diag_step, 1)
                part = diag4[:, 0:3, :]
                pool.wait_ge(diag_step, 2)
                ps.affine_select(out=part, in_=part, compare_op=ALU.is_ge, fill=0.0, base=0,
                                 pattern=[[-32, 3], [-DK, 4]], channel_multiplier=1).then_inc(diag_step, 1)
                pool.wait_ge(diag_step, 3)
                ps.affine_select(out=part, in_=part, compare_op=ALU.is_ge, fill=0.0, base=DK - 1,
                                 pattern=[[32, 3], [DK, 4]], channel_multiplier=-1).then_inc(diag_step, 1)
                ps.affine_select(out=diag4[:, 3, :], in_=diag4[:, 3, :], compare_op=ALU.not_equal, fill=1.0,
                                 base=-96, pattern=[[-1, 4]], channel_multiplier=1).then_inc(diag_step, 1)

            def layer_norm(n):
                hold(pool, ln_mean, TILES * (n + 1))
                ps.tensor_scalar(var_eps[:, :], meanvar[:, :, 1], EPS, None, ALU.add).then_inc(eps_added, 1)
                pool.wait_ge(eps_added, done(n))
                ps.tensor_tensor(rstd[:, :], var_eps[:, :], minus_half[:, :], ALU.pow).then_inc(rstd_done, 1)

            def route_norm(s, g):
                n = HGROUPS * s + g
                pool.wait_ge(r_mean, TILES * (n + 1))
                ps.tensor_scalar(r_var_eps[:, :], r_meanvar[:, g, :, 1], EPS, None, ALU.add)\
                    .then_inc(r_eps_added, 1)
                pool.wait_ge(r_eps_added, done(n))
                ps.tensor_tensor(r_rstd[:, g, :], r_var_eps[:, :], minus_half[:, :], ALU.pow)\
                    .then_inc(r_rstd_done, 1)

            def scatter(s, t):
                if t == 0:
                    pool.wait_ge(rows_done, s + 1)
                    pool.wait_ge(xs_lo, HGROUPS * (s + 1))
                    if s == 0:
                        pool.wait_ge(zeroed, 32)
                    if s >= 2:
                        for q in range(D_IO):
                            pool.wait_ge(xg_loaded[q], 16 * io_use(s - 1, q, 0))
                for k in range(2):
                    ps.indirect_dma_start(
                        out=sorted_x[s % 2],
                        out_offset=bass.IndirectOffsetOnAxis(ap=row[:, s % 2, k, t:t + 1], axis=0),
                        in_=xs[:, s % 2, t, :], in_offset=None).then_inc(scattered[s % 2], 16)

            def gather(s, t):
                if t == 0:
                    for q in range(D_IO):
                        pool.wait_ge(y_stored[q], 16 + 16 * io_use(s + 1, q, 0))
                before_this = HT * s + t - D_YG
                if t >= D_YG:
                    pool.wait_ge(x_sum, 2 * (before_this + 1))
                elif s > 0:
                    pool.wait_ge(x_sum, 2 * HT * s)
                for k in range(2):
                    ps.indirect_dma_start(
                        out=yg[:, t % D_YG, k, :], out_offset=None, in_=sorted_y[s % 2],
                        in_offset=bass.IndirectOffsetOnAxis(ap=row[:, s % 2, k, t:t + 1], axis=0))\
                        .then_inc(gathered[t % D_YG], 16)

            def gather_at(t, buf):
                hold(pool, x_sum, 2 * (HT + t - D_YG + 1))
                ps.tensor_copy(row_now[:, buf, :], row[:, 1, :, bass.ds(t, 1)].rearrange("p k a -> p (k a)"))\
                    .then_inc(row_copied, 1)
                hold(pool, row_copied, t + 1)
                for k in range(2):
                    ps.indirect_dma_start(
                        out=yg[:, buf, k, :], out_offset=None, in_=sorted_y[1],
                        in_offset=bass.IndirectOffsetOnAxis(ap=row_now[:, buf, k:k + 1], axis=0))\
                        .then_inc(gathered[buf], 16)

            for g in range(HGROUPS):
                route_norm(0, g)
                if g == 1:
                    routing_constants()
            attention_constants()
            for t in range(HT):
                scatter(0, t)
                if t % 3 == 1 and t < 3 * HGROUPS:
                    route_norm(1, t // 3)
            for t in range(HT):
                scatter(1, t)
            for t in range(HT):
                gather(0, t)
            layer_norm(0)
            layer_norm(1)

            def clamp(b, q):
                hold(pool, s_reduced, done(12 * b + 11, D_S))
                ps.tensor_scalar(negmax_h[:, q % 2], negmax[:, q % 2], -MLIMIT, MLIMIT, ALU.max, ALU.min)\
                    .then_inc(clamp_done, 1)

            def step(b, q, G, scores=True, ln=True, gathers=(), route=None, scatters=()):
                for t, buf in gathers:
                    gather_at(t, buf)
                for hg in range(HG):
                    if hg == 0 and route is not None:
                        route_norm(*route)
                    if hg == 1 and q % 2 == 0 and ln:
                        layer_norm(G + 2)
                    if hg == 2 and scores:
                        clamp(b + 1, q + 1)
                    if scatters:
                        for t in scatters[hg]:
                            scatter(2, t)

            for q in range(D_IO):
                pool.wait_ge(y_stored[q], 16 + 16 * io_use(2, q, 0))
            clamp(0, 0)
            step(0, 0, 0)
            with pool.Fori(0, FIRST // 4) as i:
                for q in range(1, 5):
                    step(4 * i + q, q, 2 * i + q // 2, gathers=[(t, buf) for t, buf, _ in add_units(i, q)])
            t = 0
            for b in range(FIRST, batches):
                scatters = []
                if b >= ROUTED:
                    for n in (0, 0, 2, 2) if b == ROUTED else (1, 2, 2, 1):
                        scatters.append(range(t, t + n))
                        t += n
                step(b, b % 4, b // 2, scores=b + 1 < batches, ln=b // 2 + 2 < groups,
                     route=route_of(b), scatters=scatters)
            route_norm(3, HGROUPS - 1)
            while t < HT:
                scatter(2, t)
                t += 1
            for t in range(HT):
                scatter(3, t)
            for s in (2, 3):
                for t in range(HT):
                    gather(s, t)

        @block.scalar
        def _(act):
            s_ = nc.scalar
            act.sem_inc(silu_done, D_H)
            act.sem_inc(hi_done, D_H)
            act.sem_inc(y_copied, D_Y)
            for q in range(D_IO):
                act.sem_inc(y_stored[q], 16)
            act.sem_inc(exp_done, D_ST)
            act.sem_inc(o_copied, D_O)

            act.wait_ge(small_loaded, 16)
            s_.activation(wsh[:, :], wsmall_f[:, :], ACT.Copy, scale=WSCALE).then_inc(w_hi, 1)

            def x_high(use, par):
                act.wait_ge(m0_ready, done(use))
                s_.activation(xh[:, par, :], bank[:, B_M0, :], ACT.Copy).then_inc(m0_hi, 1)

            def rows_high(s, g):
                s_.activation(xs[:, s % 2, bass.ds(TILES * g, TILES), 0:D], r_xn[:, :, :], ACT.Copy)\
                    .then_inc(xs_hi, 1)

            def transposed(s, g):
                act.wait_ge(m0_ready, done(m0_route(s, g)))
                s_.activation(xth[:, :, :].rearrange("p a b -> p (a b)"), bank[:, B_M0, :].bitcast(F16),
                              ACT.Copy).then_inc(m0_freed, 1)

            def tanh(s):
                act.wait_ge(gate_diff, s + 1)
                s_.activation(top[:, 5, :], top[:, 4, :], ACT.Tanh, scale=0.5 / WSCALE).then_inc(gate_tanh, 1)

            def rows_and_transposed(s, g):
                act.wait_ge(r_xn_done, TILES * (HGROUPS * s + g + 1))
                rows_high(s, g)
                transposed(s, g)

            def route(s):
                with act.Fori(0, HGROUPS) as g:
                    rows_and_transposed(s, g)
                tanh(s)

            def x_copy(s, i, q):
                n = NT * s + i
                act.wait_ge(t_ready, done(n))
                if not isinstance(i, int):
                    act.wait_ge(h3_ready, n - 1)
                elif n >= 2:
                    act.wait_ge(h3_ready, n - min(i, 1))
                s_.activation(xt[:, q % 2].rearrange("p a b -> p (a b)"), t_bank(q), ACT.Copy)\
                    .then_inc(t_copied, 1)

            def hidden(s, i, q, nxt=None):
                n = NT * s + i
                act.wait_ge(h1_ready, done(n))
                act.wait_ge(prod_done, freed(n))
                s_.activation(silu[:, q % D_H], bank[:, B_H1 + q % 2, :], ACT.Silu, scale=1.0 / WSCALE)\
                    .then_inc(silu_done, 1)
                if nxt is not None:
                    x_copy(s, *nxt)
                act.wait_ge(prod_done, done(n, D_H))
                act.wait_ge(y_ready, freed(n))
                s_.activation(hidh[:, q], prod[:, q % D_H], ACT.Copy).then_inc(hi_done, 1)

            def y_copy(s, q, j):
                i = 4 * j + q
                act.wait_ge(y_ready, done(NT * s + i, D_HID))
                act.wait_ge(y_stored[q], 16 + 16 * io_use(s, q, j))
                s_.activation(yb[:, q].rearrange("p a b -> p (a b)"), bank[:, B_Y, 0:2 * D],
                              ACT.Copy).then_inc(y_copied, 1)

            def experts(s, beside=None):
                x_copy(s, 0, 0)
                x_copy(s, 1, 1)
                for i in range(LAG):
                    hidden(s, i, i, (i + 2, i + 2) if i + 2 <= LAG else None)
                    if beside:
                        beside(i)

                def four(j, last=False):
                    for u in range(4):
                        y_copy(s, u, j)
                        i = 4 * j + u + LAG
                        hidden(s, i, (u + LAG) % 4, None if last and u == 3 else (i + 1, u))
                        if beside and isinstance(j, int):
                            beside(4 * j + u + LAG)

                rounds(act, s, four)
                for q in range(LAG):
                    y_copy(s, q, LOOPS)
                    if beside:
                        beside(NT + q)

            route(0)
            for k in range(4):
                rows_and_transposed(1, k)
                for n, w in enumerate((w1h, w3h, w2h)):
                    act.wait_ge(w_loaded[3 * k + n], 16)
                    s_.activation(w[:, k * 512:(k + 1) * 512], wstage[:, 3 * k + n, :], ACT.Copy,
                                  scale=WSCALE).then_inc(w_hi, 1)
            tanh(1)
            experts(0)

            def q_high(G, par):
                act.wait_ge(m0_ready, done(m0_use(G, 1)))
                s_.activation(qksplit[:, par, 1, :], bank[:, B_M0, :], ACT.Copy, scale=1.0 / WSCALE)\
                    .then_inc(m0_hi, 1)

            def k_high(G, par):
                act.wait_ge(m0_ready, done(m0_use(G, 2)))
                s_.activation(qksplit[:, par, 2, :], bank[:, B_M0, :], ACT.Copy, scale=1.0 / WSCALE)\
                    .then_inc(m0_hi, 1)

            def v_copy(G, par):
                act.wait_ge(m0_ready, done(m0_use(G, 3)))
                s_.activation(vaug[:, par, :, :, 0:DK],
                             bank[:, B_M0, :].rearrange("p (t h d) -> p t h d", t=TILES, d=DK),
                             ACT.Copy, scale=1.0 / WSCALE).then_inc(m0_freed, 1)

            def o_copy(b, q, half):
                act.wait_ge(pv_done, done(4 * b + 2 * half + 1, D_PT))
                s_.activation(ot[:, q % 2, 2 * half:2 * half + 2, :].rearrange("p a b -> p (a b)"),
                             bank[:, B_O, :], ACT.Copy).then_inc(o_copied, 1)

            def place_max(b, q, use):
                act.wait_ge(m1_ready, done(use))
                e = q % 2
                s_.activation(zc[96:100, (q // 2) % 2, 0, :, e * SEQ:(e + 1) * SEQ],
                              bank[96:100, B_M1, :].bitcast(F16).rearrange("p (g q) -> p g q", g=HG),
                              ACT.Copy).then_inc(m1_freed, 1)

            def o_high(u0):
                act.wait_ge(m1_ready, done(u0 + 2))
                s_.activation(oh[:, :], bank[:, B_M1, 0:SEQ], ACT.Copy).then_inc(oh_done, 1)

            def step(b, q, G, prev=True, route=None):
                for u in range(12):
                    hg, a = divmod(u, 3)
                    v = 4 * b + hg
                    if a == 0:
                        act.wait_ge(pv_done, freed(v))
                    act.wait_ge(st_ready, done(12 * b + u))
                    s_.activation(pt[:, hg, 512 * a:512 * a + 512], bank[:, B_ST + a, :], ACT.Exp,
                                 scale=SM_SCALE).then_inc(exp_done, 1)
                    if u == 2 and prev:
                        o_copy(b - 1, q - 1, 1)
                    if u == 8 and prev:
                        o_high(m1_use(b))
                    if u == 9:
                        o_copy(b, q, 0)
                    if u == 10:
                        if b_ok(b + 1):
                            place_max(b + 1, q + 1, max_use(b))
                        else:
                            no_use(act, max_use(b), m1_freed)
                    if q % 2 == 0 and u == 5 and G_ok(G + 1):
                        v_copy(G + 1, (q // 2 + 1) % 2)
                    if q % 2 == 1 and G_ok(G + 2):
                        if u == 2:
                            q_high(G + 2, (q // 2) % 2)
                        if u == 6:
                            k_high(G + 2, (q // 2) % 2)
                    if route is not None:
                        if u == 5:
                            act.wait_ge(r_xn_done, TILES * (HGROUPS * route[0] + route[1] + 1))
                            rows_high(*route)
                        if u == 7 and b == ROUTED:
                            tanh(2)
                        if u == 8:
                            transposed(*route)
                    if q % 2 == 0 and u == 11 and G_ok(G + 2):
                        x_high(m0_use(G + 2), (q // 2) % 2)

            def first_groups(slot):
                if slot == NT - 2:
                    x_high(m0_use(0), 0)
                if slot == NT - 1:
                    q_high(0, 0)
                if slot == NT:
                    k_high(0, 0)
                if slot == NT + 1:
                    v_copy(0, 0)
                if slot == NT + 2:
                    x_high(m0_use(1), 1)

            act.wait_ge(vaug_set, 2)
            experts(1, first_groups)
            q_high(1, 1)
            k_high(1, 1)
            place_max(0, 0, 0)
            step(0, 0, 0, prev=False)
            with act.Fori(0, FIRST // 4) as i:
                for q in range(1, 5):
                    step(4 * i + q, q, 2 * i + q // 2)
            for b in range(FIRST, batches):
                step(b, b % 4, b // 2, route=route_of(b))
            o_copy(batches - 1, 3, 1)
            o_high(M1_TAIL)

            act.wait_ge(r_xn_done, TILES * HGROUPS * 4)
            rows_high(3, HGROUPS - 1)

            def last_group(slot):
                if slot == 1:
                    transposed(3, HGROUPS - 1)
                if slot == 4:
                    tanh(3)

            experts(2, last_group)
            experts(3)

        @block.vector
        def _(dve):
            v_ = nc.vector
            dve.sem_inc(prod_done, D_H)
            dve.sem_inc(lo_done, D_H)
            dve.sem_inc(s_reduced, D_S)

            dve.wait_ge(w_hi, 1)
            v_.scalar_tensor_tensor(wsl[:, :], wsmall_f[:, :], WSCALE, wsh[:, :], ALU.mult, ALU.subtract)\
                .then_inc(w_lo, 1)

            def x_tile(t, n=1):
                return X[:, bass.ds(t * D, n * D)]

            def ln_stat(n, t, tile):
                v_.bn_stats(stats[:, t, :], x_tile(tile)).then_inc(ln_stats, 1)

            def ln_mean_of(n, t):
                hold(dve, ln_stats, TILES * n + t + 1)
                v_.bn_aggr(meanvar[:, t, :], stats[:, t, :]).then_inc(ln_mean, 1)

            def normalise(n, t, tile):
                if t == 0:
                    dve.wait_ge(rstd_done, done(n))
                v_.tensor_scalar(xn[:, t, :], x_tile(tile), meanvar[:, t, 0:1], rstd[:, t:t + 1],
                                 ALU.subtract, ALU.mult).then_inc(xn_done, 1)

            def x_low(n_hi, use, par):
                dve.wait_ge(m0_hi, done(n_hi))
                v_.tensor_tensor(xl[:, par, :], bank[:, B_M0, :], xh[:, par, :], ALU.subtract)\
                    .then_inc(m0_freed, 1)

            def hi_use(g):
                return 3 * g

            def row_stats(s, g, tiles):
                for t in tiles:
                    v_.bn_stats(r_stats[:, g, t, :], x_tile(HT * (s % 2) + TILES * g + t)).then_inc(r_stated, 1)

            def row_means(s, g):
                for t in range(TILES):
                    hold(dve, r_stated, TILES * (HGROUPS * s + g) + t + 1)
                    v_.bn_aggr(r_meanvar[:, g, t, :], r_stats[:, g, t, :]).then_inc(r_mean, 1)

            def normalise_rows(s, g):
                n = HGROUPS * s + g
                dve.wait_ge(r_rstd_done, done(n))
                if not isinstance(n, int) or n > 0:
                    dve.wait_ge(xs_lo, n)
                for t in range(TILES):
                    v_.tensor_scalar(r_xn[:, t, :], x_tile(HT * (s % 2) + TILES * g + t),
                                     r_meanvar[:, g, t, 0:1], r_rstd[:, g, t:t + 1], ALU.subtract, ALU.mult)\
                        .then_inc(r_xn_done, 1)

            def rows_low(s, g):
                dve.wait_ge(xs_hi, HGROUPS * s + g + 1)
                sl = bass.ds(TILES * g, TILES)
                v_.tensor_tensor(xs[:, s % 2, sl, D:2 * D], r_xn[:, :, :], xs[:, s % 2, sl, 0:D],
                                 ALU.subtract).then_inc(xs_lo, 1)

            def logits(s, g):
                dve.wait_ge(m0_ready, done(m0_route(s, g) + 1))
                v_.tensor_copy(logit[:, bass.ds(TILES * g, TILES), :],
                               bank[:, B_M0, 0:TILES * E].rearrange("p (a b) -> p a b", b=E))\
                    .then_inc(m0_freed, 1)

            def statistics(s, g):
                row_stats(s, g, range(TILES))
                row_means(s, g)

            def parts(s, g):
                normalise_rows(s, g)
                if g + 1 < HGROUPS:
                    if s == 0 and g == 0:
                        dve.wait_ge(x_rest, 16 * (groups - 1))
                    statistics(s, g + 1)
                if g > 0:
                    logits(s, g - 1)
                rows_low(s, g)

            def bc(col):
                return col.unsqueeze(2).broadcast_to([P, HT, E])

            def routing(s):
                count = [0]

                def link(ins):
                    ins.then_inc(gate_step, 1)
                    count[0] += 1
                    dve.wait_ge(gate_step, ROUTE_STEPS * s + count[0])

                def first(src, peak, which, hot):
                    link(v_.tensor_reduce(top[:, peak, :], src[:, :, :], AX.X, ALU.max))
                    link(v_.tensor_tensor(score[:, :, :], src[:, :, :], bc(top[:, peak, :]), ALU.is_equal))
                    link(v_.tensor_tensor(score[:, :, :], score[:, :, :], rank[:, :, :], ALU.mult))
                    link(v_.tensor_reduce(top[:, which, :], score[:, :, :], AX.X, ALU.max))
                    link(v_.tensor_tensor(hot[:, :, :], score[:, :, :], bc(top[:, which, :]), ALU.is_equal))

                def highest():
                    dve.wait_ge(m0_freed, m0_route(s, HGROUPS - 1) + 2)
                    first(logit, 0, 1, hot1)

                def second():
                    link(v_.scalar_tensor_tensor(masked[:, :, :], hot1[:, :, :], NEG, logit[:, :, :],
                                                 ALU.mult, ALU.add))
                    first(masked, 2, 3, hot2)
                    v_.tensor_tensor(chosen[:, 0:HT, :], hot1[:, :, :], hot2[:, :, :], ALU.add)\
                        .then_inc(hot_done, 1)
                    v_.tensor_tensor(top[:, 4, :], top[:, 0, :], top[:, 2, :], ALU.subtract)\
                        .then_inc(gate_diff, 1)

                def places():
                    dve.wait_ge(m0_ready, done(m0_sums(s)))
                    total = bank[:, B_M0, HT * E:(HT + 1) * E]
                    link(v_.tensor_tensor(over[:, :, :], total.unsqueeze(2).broadcast_to([P, E, ETILES]),
                                          bounds[:, :, :], ALU.is_gt))
                    link(v_.tensor_reduce(ntiles[:, :], over[:, :, :], AX.X, ALU.add))
                    link(v_.tensor_tensor(shares[:, :, :], ntiles[:, :].unsqueeze(1).broadcast_to([P, E, E]),
                                          before[:, :, :], ALU.mult))
                    link(v_.tensor_reduce(start[:, :], shares[:, :, :], AX.X, ALU.add))
                    v_.scalar_tensor_tensor(place[:, :, :],
                                            start[:, :].unsqueeze(1).broadcast_to([P, HT, E]), float(SLOTS),
                                            bank[:, B_M0, 0:HT * E].rearrange("p (a b) -> p a b", b=E),
                                            ALU.mult, ALU.add).then_inc(m0_freed, 1)

                def rows_of_tokens():
                    dve.wait_ge(m0_freed, m0_sums(s) + 1)
                    for k, hot in enumerate((hot1, hot2)):
                        link(v_.tensor_tensor(score[:, :, :], hot[:, :, :], place[:, :, :], ALU.mult))
                        link(v_.tensor_reduce(rowf[:, k, :], score[:, :, :], AX.X, ALU.add))
                    v_.tensor_scalar(row[:, s % 2], rowf[:, :, :], 1.0, None, ALU.mult).then_inc(rows_done, 1)

                def tile_experts():
                    link(v_.tensor_tensor(passed[:, :, :], tile_no[:, :, :],
                                          start[:, 1:E].unsqueeze(1).broadcast_to([P, NT + 1, E - 1]),
                                          ALU.is_ge))
                    link(v_.tensor_reduce(expert[:, :], passed[:, :, :], AX.X, ALU.add))
                    v_.tensor_scalar(woffset[:, s % 2, :], expert[:, :], float(HID), None, ALU.mult)\
                        .then_inc(tiles_done, 1)

                def weights():
                    dve.wait_ge(gate_tanh, s + 1)
                    link(v_.tensor_scalar(weight[:, s % 2, 0, :], top[:, 5, :], 1.0, 0.25 / WSCALE,
                                          ALU.add, ALU.mult))
                    link(v_.tensor_scalar(weight[:, s % 2, 1, :], top[:, 5, :], -1.0, -0.25 / WSCALE,
                                          ALU.add, ALU.mult))
                    assert count[0] == ROUTE_STEPS

                return highest, second, places, rows_of_tokens, tile_experts, weights

            def route(s):
                statistics(s, 0)
                for g in range(HGROUPS):
                    parts(s, g)
                logits(s, HGROUPS - 1)
                if s == 0:
                    dve.wait_ge(consts, 19)
                for part in routing(s):
                    part()

            def low_part(s, q, j):
                n = NT * s + 4 * j + q
                dve.wait_ge(hi_done, done(n, D_H))
                dve.wait_ge(y_ready, freed(n))
                v_.tensor_tensor(hidl[:, q], prod[:, q % D_H], hidh[:, q], ALU.subtract)\
                    .then_inc(lo_done, 1)

            def product(s, q, j):
                i = 4 * j + q
                n = NT * s + i
                dve.wait_ge(h3_ready, done(n))
                dve.wait_ge(silu_done, done(n, D_H))
                dve.wait_ge(hi_done, freed(n))
                dve.wait_ge(lo_done, freed(n))
                v_.scalar_tensor_tensor(prod[:, q % D_H], bank[:, B_H3 + q % 2, :], 1.0 / WSCALE,
                                        silu[:, q % D_H], ALU.mult, ALU.mult).then_inc(prod_done, 1)

            def add(s, t, buf, uses):
                dve.wait_ge(gathered[buf], 32 * (unit_count(s, buf) + uses + 1))
                tile = HT * (s % 2) + t
                for k in range(2):
                    v_.scalar_tensor_tensor(x_tile(tile), yg[:, buf, k, :],
                                            weight[:, s % 2, k, bass.ds(t, 1)],
                                            x_tile(tile), ALU.mult, ALU.add).then_inc(x_sum, 1)
                    dve.wait_ge(x_sum, 2 * (HT * s + t) + k + 1)

            def experts(s, side, beside=None):
                for i in range(LAG):
                    if i > 0:
                        low_part(s, i - 1, 0)
                    product(s, i, 0)
                    if beside:
                        beside(i)

                def four(j, last=False):
                    for u in range(4):
                        q, jq = (u + LAG) % 4, (j if u == 0 else j + 1)
                        low_part(s, (u + LAG - 1) % 4, j if u < 2 else j + 1)
                        product(s, q, jq)
                        if side and not last:
                            add(s - 1, 4 * j + u, u, j)
                        if beside and isinstance(j, int):
                            beside(4 * j + u + LAG)

                rounds(dve, s, four)
                low_part(s, LAG - 1, LOOPS)

            dve.wait_ge(x_first, 16)
            route(0)
            statistics(1, 0)
            for k in range(4):
                parts(1, k)
                for n, (hi, lo) in enumerate(((w1h, w1l), (w3h, w3l), (w2h, w2l))):
                    cols = slice(k * 512, (k + 1) * 512)
                    dve.wait_ge(w_hi, 2 + 3 * k + n)
                    v_.scalar_tensor_tensor(lo[:, cols], wstage[:, 3 * k + n, :], WSCALE, hi[:, cols],
                                            ALU.mult, ALU.subtract).then_inc(w_lo, 1)
            logits(1, HGROUPS - 1)
            for part in routing(1):
                part()
            experts(0, False)

            def q_low(G, par):
                dve.wait_ge(m0_hi, done(3 * G + 1))
                v_.scalar_tensor_tensor(qksplit[:, par, 0, :], bank[:, B_M0, :], 1.0 / WSCALE,
                                        qksplit[:, par, 1, :], ALU.mult, ALU.subtract).then_inc(m0_freed, 1)

            def k_low(G, par):
                dve.wait_ge(m0_hi, done(3 * G + 2))
                v_.scalar_tensor_tensor(qksplit[:, par, 3, :], bank[:, B_M0, :], 1.0 / WSCALE,
                                        qksplit[:, par, 2, :], ALU.mult, ALU.subtract).then_inc(m0_freed, 1)

            def row_max(b, q, k):
                hg, kind = divmod(k, 3)
                dve.wait_ge(s_ready, done(12 * b + k))
                src = bank[:, B_S + k % 2, :]
                if kind == 0:
                    dst = negmax[:, q % 2, 0, 4 * hg:4 * hg + 4]
                    src = src.rearrange("p (h k) -> p h k", k=P)
                else:
                    h0 = 4 * hg + 2 * (kind - 1)
                    dst = negmax[:, q % 2, 1, h0:h0 + 2]
                    src = src.rearrange("p (h k) -> p h k", k=SEQ)
                v_.tensor_reduce(dst, src, AX.X, ALU.max, negate=True).then_inc(s_reduced, 1)

            def block_diagonal(G, par, half, heads=range(4)):
                dve.wait_ge(zc_done[half], 96 * (G + 1))
                hgs = slice(2 * half, 2 * half + 2)
                for j in heads:
                    v_.tensor_scalar(zk[:, par, hgs, j, :], zc[:, par, 1, hgs, :], diag[:, j:j + 1], None,
                                     ALU.mult).then_inc(zk_done, 1)

            def o_norm(b, u0, qb):
                use = u0 + qb
                view = bank[:, B_M1, :].rearrange("p (h r) -> p h r", r=32)
                dve.wait_ge(m1_ready, done(use))
                v_.reciprocal(rden[:, qb, :], view[:, :, DK]).then_inc(rden_done, 1)
                dve.wait_ge(rden_done, 2 * (b - 1) + qb + 1)
                v_.tensor_tensor(on[:, qb, :].rearrange("p (h d) -> p h d", d=DK), view[:, :, 0:DK],
                                 rden[:, qb, :].unsqueeze(2).broadcast_to([P, HEADS, DK]), ALU.mult)\
                    .then_inc(m1_freed, 1)

            def o_low(b):
                dve.wait_ge(oh_done, b)
                v_.tensor_tensor(ol[:, :], bank[:, B_M1, 0:SEQ], oh[:, :], ALU.subtract).then_inc(m1_freed, 1)

            def x_add(b, u0, tail=False):
                dve.wait_ge(m1_ready, done(u0 + (3 if tail else 4)))
                v_.scalar_tensor_tensor(x_tile(2 * (b - 1), 2), bank[:, B_M1, 0:2 * D], 1.0 / WSCALE,
                                        x_tile(2 * (b - 1), 2), ALU.mult, ALU.add).then_inc(m1_freed, 1)

            def step(b, q, G, prev=True, adds=(), route=None):
                par = (q // 2 + 1) % 2
                for k in range(12):
                    ahead = score_bank(b, q, k)
                    if ahead is not None:
                        row_max(*ahead)
                    if prev and k == 5:
                        o_norm(b, m1_use(b), 0)
                    if prev and k == 7:
                        o_norm(b, m1_use(b), 1)
                    if prev and k == 9:
                        o_low(b)
                    if q % 2 == 1 and G_ok(G + 2):
                        if k == 3:
                            q_low(G + 2, (q // 2) % 2)
                        if k == 7:
                            k_low(G + 2, (q // 2) % 2)
                    if q % 2 == 0 and k in BD_AT and G_ok(G + 1):
                        half, part = divmod(BD_AT.index(k), 2)
                        block_diagonal(G + 1, par, half, (2 * part, 2 * part + 1))
                    if k in (3, 8) and len(adds) > (k == 8):
                        add(1, *adds[k == 8])
                    if route is not None:
                        if k == 0:
                            dve.wait_ge(m1_freed, m1_use(2 * (b - FIRST) + 2) + 5)
                            row_stats(*route, range(0, 2))
                        if k == 1:
                            row_stats(*route, range(2, TILES))
                        if k == 2:
                            row_means(*route)
                        if k == 4:
                            normalise_rows(*route)
                        if k == 6:
                            rows_low(*route)
                        if k == 10:
                            logits(*route)
                    if isinstance(b, int) and b == ROUTED and k in ROUTING_AT:
                        routing_2[ROUTING_AT.index(k)]()
                    if q % 2 == 0 and G_ok(G + 2):
                        n = G + 2
                        tile = TILES * (G + 2)
                        if k in (0, 1, 2, 3):
                            ln_stat(n, k, tile + k)
                        if k in (1, 2, 3, 4):
                            ln_mean_of(n, k - 1)
                        if k in (6, 10):
                            for t in (0, 1) if k == 6 else (2, 3):
                                normalise(n, t, tile + t)
                if q % 2 == 0 and G_ok(G + 2):
                    x_low(hi_use(G + 2), m0_use(G + 2), (q // 2) % 2)
                if prev:
                    x_add(b, m1_use(b))
                else:
                    no_use(dve, max_use(b) + 1, m1_freed)
            routing_2 = routing(2)
            ROUTING_AT = (0, 1, 5, 7, 9, 11)
            BD_AT = (4, 5, 8, 9)

            def attention_norm(g):
                for t in range(TILES):
                    ln_stat(g, t, TILES * g + t)
                for t in range(TILES):
                    ln_mean_of(g, t)

            def first_groups(slot):
                if slot == NT - 4:
                    attention_norm(0)
                if slot == NT - 3:
                    for t in range(TILES):
                        normalise(0, t, t)
                if slot == NT - 2:
                    x_low(hi_use(0), m0_use(0), 0)
                if slot == NT - 1:
                    q_low(0, 0)
                    attention_norm(1)
                    k_low(0, 0)

            experts(1, True, first_groups)
            for t in range(TILES):
                normalise(1, t, TILES + t)
            x_low(hi_use(1), m0_use(1), 1)
            dve.wait_ge(y_copied, done(2 * NT - 1, D_Y))
            for q in range(D_IO):
                dve.wait_ge(y_stored[q], 16 + 16 * io_use(2, q, 0))
            q_low(1, 1)
            k_low(1, 1)
            dve.wait_ge(diag_step, 5)
            v_.tensor_reduce(diag[:, :], diag4[:, :, :].rearrange("p r j -> p j r"), AX.X, ALU.max)\
                .then_inc(diag_done, 1)
            dve.wait_ge(diag_done, 1)
            for half in range(2):
                block_diagonal(0, 0, half)
                for k in range(6 * half, 6 * half + 6):
                    row_max(0, 0, k)
            for k in range(AHEAD):
                row_max(1, 1, k)
            step(0, 0, 0, prev=False)
            with dve.Fori(0, FIRST // 4) as i:
                for q in range(1, 5):
                    step(4 * i + q, q, 2 * i + q // 2, adds=add_units(i, q))
            for b in range(FIRST, batches):
                step(b, b % 4, b // 2, route=route_of(b))
            o_norm(batches, M1_TAIL, 0)
            o_norm(batches, M1_TAIL, 1)
            o_low(batches)
            x_add(batches, M1_TAIL, tail=True)
            dve.wait_ge(m1_freed, M1_TAIL + 4)
            statistics(3, HGROUPS - 1)
            normalise_rows(3, HGROUPS - 1)
            routing_3 = routing(3)
            ROUTING_3_AT = (2, 3, 4, 5, 6, 7)

            def last_group(slot):
                if slot == 0:
                    rows_low(3, HGROUPS - 1)
                if slot == 2:
                    logits(3, HGROUPS - 1)
                if slot in ROUTING_3_AT:
                    routing_3[ROUTING_3_AT.index(slot)]()

            experts(2, False, last_group)
            experts(3, True)
            with dve.Fori(0, HT // D_YG) as j:
                for u in range(D_YG):
                    add(3, D_YG * j + u, u, j)

        @block.tensor
        def _(pe):
            t_ = nc.tensor
            pe.sem_inc(y_ready, D_HID)
            pe.sem_inc(pv_done, D_PT)

            def x_transpose(n, use):
                pe.wait_ge(xn_done, TILES * (n + 1))
                if not isinstance(use, int) or use > 0:
                    pe.wait_ge(m0_freed, use)
                for t in range(TILES):
                    last = t_.transpose(bank[:, B_M0, t * P:(t + 1) * P], xn[:, t, :], ident[:, :])
                last.then_inc(m0_ready, 1)

            def split_product(dst, ah, al, bh, bl):
                t_.matmul(dst, ah, bh, start=True, stop=False)
                t_.matmul(dst, ah, bl, start=False, stop=False)
                return t_.matmul(dst, al, bh, start=False, stop=True)

            def transpose_rows(s, g):
                use = m0_route(s, g)
                pe.wait_ge(xs_lo, HGROUPS * s + g + 1)
                if not isinstance(use, int) or use > 0:
                    pe.wait_ge(m0_freed, use)
                dst = bank[:, B_M0, :].bitcast(F16)
                for h in range(2):
                    for t in range(TILES):
                        c0 = h * GTOK + t * P
                        last = t_.transpose(dst[:, c0:c0 + P],
                                            xs[:, s % 2, bass.ds(TILES * g + t, 1), h * D:(h + 1) * D]
                                            .rearrange("p a b -> p (a b)"), ident_h[:, :])
                last.then_inc(m0_ready, 1)

            def gate(s, g):
                use = m0_route(s, g) + 1
                pe.wait_ge(m0_freed, use)
                gate = slice(4 * D, 4 * D + E)
                for t in range(TILES):
                    xh_, xl_ = xth[:, 0, t * P:(t + 1) * P], xth[:, 1, t * P:(t + 1) * P]
                    dst = bank[:, B_M0, t * E:(t + 1) * E]
                    t_.matmul(dst, xh_, wsh[:, gate], start=True, stop=False)
                    t_.matmul(dst, xh_, wsl[:, gate], start=False, stop=False)
                    t_.matmul(dst, xl_, wsh[:, gate], start=False, stop=False)
                    last = t_.matmul(dst, xl_, wsl[:, gate], start=False, stop=True)
                last.then_inc(m0_ready, 1)

            def sums(s):
                pe.wait_ge(hot_done, s + 1)
                pe.wait_ge(m0_freed, m0_sums(s))
                dst = bank[:, B_M0, 0:(HT + 1) * E]
                t_.matmul(dst, earlier[:, :], chosen[:, :, :], start=True, stop=False, skip_group_check=True)
                for t in range(HT):
                    last = t_.matmul(dst[:, (t + 1) * E:], ones_b[:, :],
                                     chosen[:, t, :].unsqueeze(1).broadcast_to([P, HT - t, E]),
                                     start=False, stop=t == HT - 1, skip_group_check=True)
                last.then_inc(m0_ready, 1)

            def route(s):
                if s == 0:
                    pe.wait_ge(w_lo, 1)
                transpose_rows(s, 0)
                gate(s, 0)
                with pe.Fori(1, HGROUPS) as g:
                    transpose_rows(s, g)
                    gate(s, g)
                if s == 0:
                    pe.wait_ge(consts, 19)
                sums(s)

            def x_parts(s, i, q, j):
                n = NT * s + i
                pe.wait_ge(xg_loaded[q], 16 * (io_use(s, q, j) + 1))
                if not isinstance(i, int):
                    pe.wait_ge(t_copied, n - 1)
                elif n >= 2:
                    pe.wait_ge(t_copied, n - min(i, 1))
                for h in range(2):
                    for u in range(2):
                        c0 = h * SLOTS + u * P
                        last = t_.transpose(t_bank(q)[:, c0:c0 + P], xg[:, q, u, h * D:(h + 1) * D],
                                            ident_h[:, :])
                last.then_inc(t_ready, 1)

            offset_regs = [pe.alloc_register(f"weight_column{k}") for k in range(2 * D_IO)]

            def weight_columns(s, j, count):
                pe.load(offset_regs[:count], woffset[0:1, s % 2, bass.ds(4 * j, count)])
                return [pe.snap(r, min_val=0, max_val=(E - 1) * HID) for r in offset_regs[:count]]

            def up(s, i, q, off, between=None):
                n = NT * s + i
                pe.wait_ge(t_copied, done(n))
                for ready, read, b0, wh, wl in ((h1_ready, silu_done, B_H1, w1h, w1l),
                                                (h3_ready, prod_done, B_H3, w3h, w3l)):
                    pe.wait_ge(read, freed(n))
                    for c in range(2):
                        cols = bass.ds(off + c * P, P)
                        last = split_product(bank[:, b0 + q % 2, c * SLOTS:(c + 1) * SLOTS],
                                             wh[:, cols], wl[:, cols], xt[:, q % 2, 0], xt[:, q % 2, 1])
                    last.then_inc(ready, 1)
                    if between is not None and ready is h1_ready:
                        x_parts(*between)

            def down(s, q, j, off):
                i = 4 * j + q
                n = NT * s + i
                pe.wait_ge(hi_done, done(n, D_H))
                pe.wait_ge(y_copied, freed(n))
                pe.wait_ge(lo_done, done(n, D_H))
                for u in range(2):
                    dst = bank[:, B_Y, u * D:(u + 1) * D]
                    for c in range(2):
                        toks = slice(c * SLOTS + u * P, c * SLOTS + (u + 1) * P)
                        cols = bass.ds(off + c * D, D)
                        hh, hl = hidh[:, q, toks], hidl[:, q, toks]
                        t_.matmul(dst, hh, w2h[:, cols], start=c == 0, stop=False)
                        t_.matmul(dst, hh, w2l[:, cols], start=False, stop=False)
                        last = t_.matmul(dst, hl, w2h[:, cols], start=False, stop=c == 1)
                last.then_inc(y_ready, 1)

            def experts(s, beside=None):
                pe.wait_ge(tiles_done, s + 1)
                if s > 0:
                    pe.wait_ge(y_copied, done(NT * s - 1, D_Y))
                x_parts(s, 0, 0, 0)
                x_parts(s, 1, 1, 0)
                off = weight_columns(s, 0, 4)
                for i in range(LAG):
                    up(s, i, i, off[i], between=(s, i + 2, i + 2, 0) if i < 2 else None)
                    if beside:
                        beside(i)

                def four(j, last=False):
                    off = weight_columns(s, j, 8)
                    for u in range(4):
                        down(s, u, j, off[u])
                        i = 4 * j + u + LAG
                        up(s, i, (u + LAG) % 4, off[u + LAG],
                           between=None if last and u == 3 else (s, i + 1, u, j + 1))
                        if beside and isinstance(i, int):
                            beside(i)

                rounds(pe, s, four)
                off = weight_columns(s, LOOPS, 4)
                for q in range(LAG):
                    down(s, q, LOOPS, off[q])
                    if beside:
                        beside(NT + q)

            pe.wait_ge(consts, 6)
            route(0)
            route(1)
            pe.wait_ge(w_lo, 13)
            pe.wait_ge(m0_freed, M0_ATT)
            experts(0)

            WQ, WK, WV, WO = (slice(k * D, (k + 1) * D) for k in range(4))

            def project(G, par, which):
                use = m0_use(G, 1 + which)
                pe.wait_ge(m0_freed, use)
                if which < 2:
                    w = (WQ, WK)[which]
                    last = split_product(bank[:, B_M0, :], wsh[:, w], wsl[:, w], xh[:, par, :], xl[:, par, :])
                else:
                    for t in range(TILES):
                        toks = slice(t * P, (t + 1) * P)
                        last = split_product(bank[:, B_M0, toks], xh[:, par, toks], xl[:, par, toks],
                                             wsh[:, WV], wsl[:, WV])
                last.then_inc(m0_ready, 1)

            def scores(b, q, k, G_z=None):
                hg, kind = divmod(k, 3)
                par, e = (q // 2) % 2, q % 2
                if G_z is not None and k % 6 == 0:
                    pe.wait_ge(zc_done[k // 6], 96 * (G_z + 1))
                    pe.wait_ge(zk_done, 8 * G_z + 4 * (k // 6 + 1))
                pe.wait_ge(s_reduced, freed(12 * b + k))
                dst = bank[:, B_S + k % 2, :]
                q0 = e * SEQ + (0 if kind == 0 else P)
                qs = zc[0:96, par, 0, hg, q0:q0 + P]
                if kind == 0:
                    t_.matmul(dst, qs, zk[0:96, par, hg, :, e * SEQ:e * SEQ + P], start=True, stop=False)
                    t_.matmul(dst, ident_b[:, :], causal[:, :, :], start=False, stop=True)\
                        .then_inc(s_ready, 1)
                else:
                    j = 2 * (kind - 1)
                    t_.matmul(dst, qs, zk[0:96, par, hg, j:j + 2, e * SEQ:(e + 1) * SEQ],
                              start=True, stop=False, skip_group_check=True)
                    t_.matmul(dst.rearrange("p (h k) -> p h k", k=SEQ)[:, :, P:SEQ], ident_b[:, :],
                              causal[:, 0:2, :], start=False, stop=True, skip_group_check=True)\
                        .then_inc(s_ready, 1)

            def max_transpose(b, q, use):
                pe.wait_ge(clamp_done, done(b))
                if not isinstance(use, int) or use > 0:
                    pe.wait_ge(m1_freed, use)
                dst = bank[96:100, B_M1, :].bitcast(F16)
                for qb in range(2):
                    for hg in range(HG):
                        last = t_.transpose(dst[:, hg * SEQ + qb * P:hg * SEQ + qb * P + P],
                                            negmax_h[:, q % 2, qb, 4 * hg:4 * hg + 4], ident_h[:, :])
                last.then_inc(m1_ready, 1)

            def scores_t(b, q, u):
                hg, a = divmod(u, 3)
                par, e = (q // 2) % 2, q % 2
                if u == 0:
                    pe.wait_ge(m1_freed, done(0 if isinstance(b, int) and b == 0 else max_use(b - 1)))
                pe.wait_ge(exp_done, freed(12 * b + u))
                dst = bank[:, B_ST + a, :]
                k0 = e * SEQ + (0 if a < 2 else P)
                heads = (0, 1) if a == 0 else (2, 3) if a == 1 else (0, 1, 2, 3)
                nq = SEQ if a < 2 else P
                for m, j in enumerate(heads):
                    t_.matmul(dst[:, m * nq:(m + 1) * nq], zk[:, par, hg, j, k0:k0 + P],
                              zc[:, par, 0, hg, (e + 1) * SEQ - nq:(e + 1) * SEQ],
                              start=m == 0, stop=False, skip_group_check=True)
                last = t_.matmul(dst.rearrange("p (h q) -> p h q", q=nq)[:, :, 0:P], ident_b[:, :],
                                 causal_t[:, 0:len(heads), :], start=False, stop=True, skip_group_check=True)
                last.then_inc(st_ready, 1)

            def values(b, q, hg):
                v = 4 * b + hg
                par, e = (q // 2) % 2, q % 2
                pe.wait_ge(exp_done, done(3 * v + 2, D_ST))
                if hg % 2 == 0:
                    pe.wait_ge(o_copied, freed(2 * b + hg // 2))
                c0 = (hg % 2) * SEQ
                buf = pt[:, hg]
                for j in range(4):
                    t_.matmul(bank[32 * j:32 * j + 32, B_O, c0:c0 + SEQ], vaug[:, par, 2 * e, 4 * hg + j, :],
                              buf[:, j * SEQ:(j + 1) * SEQ], start=True, stop=False, skip_group_check=True)
                for j in range(4):
                    last = t_.matmul(bank[32 * j:32 * j + 32, B_O, c0 + P:c0 + SEQ],
                                     vaug[:, par, 2 * e + 1, 4 * hg + j, :],
                                     buf[:, 1024 + j * P:1024 + (j + 1) * P], start=False, stop=True,
                                     skip_group_check=True)
                last.then_inc(pv_done, 1)

            def o_back(b, q, u0, qb):
                use = u0 + qb
                pe.wait_ge(o_copied, done(2 * (b - 1) + 1, D_O))
                pe.wait_ge(m1_freed, use)
                for hg in range(HG):
                    last = t_.transpose(bank[:, B_M1, hg * P:(hg + 1) * P],
                                        ot[:, (q - 1) % 2, hg, qb * P:(qb + 1) * P], ident[:, :])
                last.then_inc(m1_ready, 1)

            def o_transpose(u0):
                use = u0 + 2
                pe.wait_ge(m1_freed, use)
                for qb in range(2):
                    last = t_.transpose(bank[:, B_M1, qb * P:(qb + 1) * P], on[:, qb, :], ident[:, :])
                last.then_inc(m1_ready, 1)

            def o_project(u0, tail=False):
                use = u0 + 3 + (0 if tail else 1)
                pe.wait_ge(m1_freed, use)
                for qb in range(2):
                    toks = slice(qb * P, (qb + 1) * P)
                    last = split_product(bank[:, B_M1, toks], oh[:, toks], ol[:, toks], wsh[:, WO], wsl[:, WO])
                last.then_inc(m1_ready, 1)

            def step(b, q, G, prev=True, route=None):
                par = (q // 2 + 1) % 2
                for u in range(12):
                    ahead = score_bank(b, q, u)
                    if ahead is not None:
                        scores(*ahead, G + 1 if ahead[1] % 2 == 0 else None)
                    scores_t(b, q, u)
                    if q % 2 == 0 and u == 4 and G_ok(G + 1):
                        project(G + 1, par, 2)
                    if q % 2 == 1 and u in (1, 5) and G_ok(G + 2):
                        project(G + 2, (q // 2) % 2, u // 5)
                    if u == 1 and prev:
                        values(b - 1, q - 1, 3)
                    if u == 4 and prev:
                        o_back(b, q, m1_use(b), 0)
                    if u == 5:
                        values(b, q, 0)
                    if u == 6 and prev:
                        o_back(b, q, m1_use(b), 1)
                    if u == 8 and prev:
                        o_transpose(m1_use(b))
                    if u == 8:
                        values(b, q, 1)
                    if route is not None:
                        if u == 3 and b == ROUTED:
                            sums(2)
                        if u == 7:
                            transpose_rows(*route)
                        if u == 9:
                            gate(*route)
                    if u == 11 and q % 2 == 0 and G_ok(G + 2):
                        x_transpose(G + 2, m0_use(G + 2))
                    if u == 10:
                        if b_ok(b + 1):
                            max_transpose(b + 1, q + 1, max_use(b))
                        else:
                            pe.wait_ge(m1_freed, max_use(b))
                            no_use(pe, max_use(b), m1_ready)
                    if u == 11:
                        values(b, q, 2)
                        if prev:
                            o_project(m1_use(b))
                        else:
                            pe.wait_ge(m1_freed, max_use(b) + 1)
                            no_use(pe, max_use(b) + 1, m1_ready)

            def first_groups(slot):
                if slot == NT - 2:
                    x_transpose(0, m0_use(0))
                if NT - 1 <= slot <= NT + 1:
                    project(0, 0, slot - (NT - 1))
                if slot == NT + 2:
                    x_transpose(1, m0_use(1))

            experts(1, first_groups)
            pe.wait_ge(y_copied, done(2 * NT - 1, D_Y))
            for which in range(2):
                project(1, 1, which)
            pe.wait_ge(vaug_set, 2)
            for k in range(12):
                scores(0, 0, k, 0)
            max_transpose(0, 0, 0)
            for k in range(AHEAD):
                scores(1, 1, k)
            step(0, 0, 0, prev=False)
            with pe.Fori(0, FIRST // 4) as i:
                for q in range(1, 5):
                    step(4 * i + q, q, 2 * i + q // 2)
            for b in range(FIRST, batches):
                step(b, b % 4, b // 2, route=route_of(b))
            values(batches - 1, 3, 3)
            o_back(batches, 0, M1_TAIL, 0)
            o_back(batches, 0, M1_TAIL, 1)
            o_transpose(M1_TAIL)
            o_project(M1_TAIL, tail=True)

            pe.wait_ge(exp_done, done(12 * batches - 1, D_ST))
            pe.wait_ge(m1_freed, M1_TAIL + 4)

            def last_group(slot):
                if slot == 1:
                    transpose_rows(3, HGROUPS - 1)
                if slot == 2:
                    gate(3, HGROUPS - 1)
                if slot == 4:
                    sums(3)

            experts(2, last_group)
            experts(3)


_INS = ("x_in", "w_up1", "w_up3", "w_down", "w_small")


def kernel(L0_attn_x, L0_attn_WQ, L0_attn_WK, L0_attn_WV, L0_attn_WO, L0_ffn_gate_w, L0_ffn_w1,
           L0_ffn_w2, L0_ffn_w3):
    import concourse.bacc as bacc
    from concourse.bass_utils import run_bass_kernel_spmd

    x = np.asarray(L0_attn_x)
    batches, seq, d = x.shape
    assert (seq, d) == (SEQ, D)
    w1 = np.asarray(L0_ffn_w1).reshape(E * HID, D).T
    w3 = np.asarray(L0_ffn_w3).reshape(E * HID, D).T
    w2 = np.asarray(L0_ffn_w2).transpose(0, 2, 1).reshape(CHUNKS, P, D).transpose(1, 0, 2).reshape(P, -1)
    small = np.concatenate([np.asarray(w) for w in (L0_attn_WQ, L0_attn_WK, L0_attn_WV, L0_attn_WO)]
                           + [np.asarray(L0_ffn_gate_w).T], axis=1)
    arrays = dict(zip(_INS, (np.ascontiguousarray(a) for a in (x.reshape(-1, D), w1, w3, w2, small))))

    nc = bacc.Bacc("TRN2", target_bir_lowering=False, num_devices=1)
    args = [nc.dram_tensor(n, arrays[n].shape, F32, kind="ExternalInput").ap() for n in _INS]
    out = nc.dram_tensor("out", (batches * SEQ, D), F32, kind="ExternalOutput").ap()
    build_macaron(nc, *args, out, batches)
    r = run_bass_kernel_spmd(nc, [arrays], core_ids=[0])
    return r.results[0]["out"].reshape(batches, SEQ, D)
```
